# Optimizing a Trainium2 kernel written in Bass

```python
import numpy as np
import jax
import jax.numpy as jnp

def _softmax(x, axis=-1):
    return jax.nn.softmax(x, axis=axis)

def _gelu(x):
    return jax.nn.gelu(x, approximate=True)

def _silu(x):
    return jax.nn.silu(x)

def _sigmoid(x):
    return jax.nn.sigmoid(x)

def _layernorm(x, axis=-1, eps=1e-05):
    m = jnp.mean(x, axis=axis, keepdims=True)
    v = jnp.var(x, axis=axis, keepdims=True)
    return (x - m) / jnp.sqrt(v + eps)

def _scatter_add(tgt, idx, src, axis=0):
    return tgt.at[idx].add(src)

def _segment_sum(src, seg, n):
    return jax.ops.segment_sum(src, seg, n)
kernel_name = 'mk_vit_tower_cls_d1_tok_img768_r4_b27b77'

def setup_inputs(seed: int=0):
    np.random.seed(seed)
    _w = jnp.asarray

    def _rec_inputs():
        import jax
        import jax.numpy as jnp
        _rk = jax.random.key(seed)
        x = -0.000348323 + 0.999952 * jax.random.normal(jax.random.fold_in(_rk, 1), (64, 3, 224, 224), jnp.float32)
        cls_tok = 0.02 * jax.random.normal(jax.random.fold_in(_rk, 5), (1, 1, 192), jnp.float32)
        return (x, cls_tok)
    x, cls_tok = _rec_inputs()

    def _L0_tok_setup():
        import jax, jax.numpy as jnp
        import numpy as np
        P = 16
        N_EMBD = 192
        key = jax.random.key(seed)
        kx, kw, kb = jax.random.split(key, 3)
        B, C, H, W = (32, 3, 96, 96)
        cpp = C * P * P
        x = jax.random.normal(kx, (B, C, H, W), dtype=jnp.float32)
        bound = 1.0 / np.sqrt(cpp)
        W_proj = jax.random.uniform(kw, (N_EMBD, cpp), minval=-bound, maxval=bound, dtype=jnp.float32)
        b_proj = jax.random.uniform(kb, (N_EMBD,), minval=-bound, maxval=bound, dtype=jnp.float32)
        return {'x': x, 'W_proj': W_proj, 'b_proj': b_proj}
    _L0_tok_all = _L0_tok_setup()
    _L0_tok_in = {k: v for k, v in _L0_tok_all.items() if k in ('W_proj', 'b_proj')}
    del _L0_tok_all

    def _L0_attn_setup():
        import jax, jax.numpy as jnp
        import numpy as np
        B, S, H = (2, 512, 192)
        E, NH, WIN = (4, 12, 64)
        HD = H // NH
        NEG = -1e+30

        def _sliding_mask(seq_len, window):
            i = jnp.arange(seq_len)
            d = i[:, None] - i[None, :]
            return (d >= 0) & (d < window)
        key = jax.random.key(seed)
        ks = jax.random.split(key, 7)
        s = 0.02
        return {'x': jax.random.normal(ks[0], (B, S, H), jnp.float32), 'wq': jax.random.normal(ks[1], (E, H, H), jnp.float32) * s, 'wk': jax.random.normal(ks[2], (E, H, H), jnp.float32) * s, 'wv': jax.random.normal(ks[3], (E, H, H), jnp.float32) * s, 'wo': jax.random.normal(ks[4], (E, H, H), jnp.float32) * s, 'w_gate': jax.random.normal(ks[5], (H, E * H), jnp.float32) * s, 'w_up': jax.random.normal(ks[6], (E, H, H), jnp.float32).reshape(H, E * H) * 0 + jax.random.normal(jax.random.fold_in(key, 7), (H, E * H), jnp.float32) * s}
    _L0_attn_all = _L0_attn_setup()
    _L0_attn_in = {k: v for k, v in _L0_attn_all.items() if k in ('wq', 'wk', 'wv', 'wo', 'w_gate', 'w_up')}
    del _L0_attn_all

    def _L0_ffn_setup():
        import jax, jax.numpy as jnp
        import numpy as np
        B, N, C, H, E = (8, 256, 192, 768, 4)
        key = jax.random.key(seed)
        ks = jax.random.split(key, 8)
        s_in = 1.0 / np.sqrt(C)
        s_h = 1.0 / np.sqrt(H)
        return {'x': jax.random.normal(ks[0], (B, N, C), dtype=jnp.float32), 'gate_w': jax.random.normal(ks[1], (C, E), dtype=jnp.float32) * 0.01, 'gate_b': jnp.zeros((E,), dtype=jnp.float32), 'gate_center': jnp.zeros((E,), dtype=jnp.float32), 'w1': jax.random.uniform(ks[2], (E, C, H), jnp.float32, -s_in, s_in), 'b1': jax.random.uniform(ks[3], (E, H), jnp.float32, -s_in, s_in), 'w2': jax.random.uniform(ks[4], (E, H, C), jnp.float32, -s_h, s_h), 'b2': jax.random.uniform(ks[5], (E, C), jnp.float32, -s_h, s_h)}
    _L0_ffn_all = _L0_ffn_setup()
    _L0_ffn_in = {k: v for k, v in _L0_ffn_all.items() if k in ('gate_w', 'gate_b', 'gate_center', 'w1', 'b1', 'w2', 'b2')}
    del _L0_ffn_all
    return {'x': x, 'cls_tok': cls_tok, 'L0_tok_W_proj': _L0_tok_in['W_proj'], 'L0_tok_b_proj': _L0_tok_in['b_proj'], 'L0_attn_wq': _L0_attn_in['wq'], 'L0_attn_wk': _L0_attn_in['wk'], 'L0_attn_wv': _L0_attn_in['wv'], 'L0_attn_wo': _L0_attn_in['wo'], 'L0_attn_w_gate': _L0_attn_in['w_gate'], 'L0_attn_w_up': _L0_attn_in['w_up'], 'L0_ffn_gate_w': _L0_ffn_in['gate_w'], 'L0_ffn_gate_b': _L0_ffn_in['gate_b'], 'L0_ffn_gate_center': _L0_ffn_in['gate_center'], 'L0_ffn_w1': _L0_ffn_in['w1'], 'L0_ffn_b1': _L0_ffn_in['b1'], 'L0_ffn_w2': _L0_ffn_in['w2'], 'L0_ffn_b2': _L0_ffn_in['b2']}

def reference(x, cls_tok, L0_tok_W_proj, L0_tok_b_proj, L0_attn_wq, L0_attn_wk, L0_attn_wv, L0_attn_wo, L0_attn_w_gate, L0_attn_w_up, L0_ffn_gate_w, L0_ffn_gate_b, L0_ffn_gate_center, L0_ffn_w1, L0_ffn_b1, L0_ffn_w2, L0_ffn_b2):
    import jax
    import jax.numpy as jnp

    def _L0_tok_ref(x, W_proj, b_proj):
        import jax, jax.numpy as jnp
        import numpy as np
        P = 16
        N_EMBD = 192
        B, C, H, W = x.shape
        p = P
        x = x.reshape(B, C, H // p, p, W // p, p).transpose(0, 1, 2, 4, 3, 5)
        x = x.transpose(0, 2, 3, 1, 4, 5).reshape(B, H // p * (W // p), C * p * p)
        return jnp.einsum('bnk,ek->bne', x, W_proj) + b_proj

    def _L0_attn_ref(x, wq, wk, wv, wo, w_gate, w_up):
        import jax, jax.numpy as jnp
        import numpy as np
        B, S, H = (2, 512, 192)
        E, NH, WIN = (4, 12, 64)
        HD = H // NH
        NEG = -1e+30

        def _sliding_mask(seq_len, window):
            i = jnp.arange(seq_len)
            d = i[:, None] - i[None, :]
            return (d >= 0) & (d < window)
        b, s, h = x.shape
        nh, hd = (NH, h // NH)
        mask = _sliding_mask(s, WIN)
        scale = jnp.float32(1.0 / np.sqrt(hd))
        outs = []
        for e in range(wq.shape[0]):
            q = (x @ wq[e].T).reshape(b, s, nh, hd).transpose(0, 2, 1, 3)
            k = (x @ wk[e].T).reshape(b, s, nh, hd).transpose(0, 2, 1, 3)
            v = (x @ wv[e].T).reshape(b, s, nh, hd).transpose(0, 2, 1, 3)
            scores = jnp.einsum('bhqd,bhkd->bhqk', q, k) * scale
            scores = jnp.where(mask, scores, NEG)
            attn = jax.nn.softmax(scores, axis=-1)
            o = jnp.einsum('bhqk,bhkd->bhqd', attn, v)
            o = o.transpose(0, 2, 1, 3).reshape(b, s, h)
            outs.append(o @ wo[e].T)
        fused = jnp.concatenate(outs, axis=-1)
        gate = jax.nn.silu(fused @ w_gate.T)
        value = fused @ w_up.T
        return gate * value

    def _L0_ffn_ref(x, gate_w, gate_b, gate_center, w1, b1, w2, b2):
        import jax, jax.numpy as jnp
        import numpy as np
        B, N, C, H, E = (8, 256, 192, 768, 4)
        b, n, c = x.shape
        scores = jnp.einsum('bnc,ce->bne', x, gate_w) + gate_b
        p_experts = jax.nn.softmax(scores - gate_center, axis=-1)
        expert = jnp.argmax(p_experts, axis=-1).reshape(-1)
        xt = x.reshape(-1, c)
        h = jax.nn.gelu(jnp.einsum('tc,ech->eth', xt, w1) + b1[:, None, :], approximate=False)
        out_all = jnp.einsum('eth,ehc->etc', h, w2) + b2[:, None, :]
        out = jnp.take_along_axis(out_all, expert[None, :, None], axis=0)[0]
        return out.reshape(b, n, c)
    h = _L0_tok_ref(x, L0_tok_W_proj, L0_tok_b_proj)
    h = jnp.concatenate([jnp.broadcast_to(cls_tok, (h.shape[0], 1, h.shape[2])), h], axis=1)
    h = h + _L0_attn_ref(_layernorm(h, axis=-1), L0_attn_wq, L0_attn_wk, L0_attn_wv, L0_attn_wo, L0_attn_w_gate, L0_attn_w_up)
    h = h + _L0_ffn_ref(_layernorm(h, axis=-1), L0_ffn_gate_w, L0_ffn_gate_b, L0_ffn_gate_center, L0_ffn_w1, L0_ffn_b1, L0_ffn_w2, L0_ffn_b2)
    return h

_drawn_inputs = setup_inputs


def setup_inputs(seed=0):
    import zlib

    import numpy as np

    out = dict(_drawn_inputs(seed))
    spreads = {'L0_ffn_gate_b': (0.0, 0.8), 'L0_ffn_gate_center': (0.0, 2.0)}
    factors = {'L0_attn_wq': 8.0,
     'L0_attn_wk': 8.0,
     'L0_attn_wv': 8.0,
     'L0_attn_wo': 8.0,
     'L0_attn_w_gate': 8.0,
     'L0_attn_w_up': 8.0,
     'L0_ffn_gate_w': 8.0,
     'L0_ffn_w1': 8.0,
     'L0_ffn_b1': 64.0,
     'L0_ffn_w2': 8.0,
     'L0_ffn_b2': 64.0}
    for name, (base, spread) in spreads.items():
        noise = np.random.default_rng([zlib.crc32(name.encode()), seed]).standard_normal(out[name].shape)
        drawn = base * np.exp(spread * noise) if base else spread * noise
        out[name] = jnp.asarray(drawn.astype(out[name].dtype))
    for name, factor in factors.items():
        out[name] = (out[name] * factor).astype(out[name].dtype)
    return out
```

```python
from contextlib import ExitStack

import concourse.bass as bass
from concourse import mybir

F32 = mybir.dt.float32
F16 = mybir.dt.float16
ALU = mybir.AluOpType
ACT = mybir.ActivationFunctionType
AX_X = mybir.AxisListType.X

IMGS = 64
PAIR = 2
STEPS = IMGS // PAIR
TOK = 197
TP = PAIR * TOK
D = 192
KB = 96
DB = D // KB
PATCH = 768
PKT = PATCH // 128
E = 4
HD = 16
G = E * D // KB
HG = KB // HD
HU = HG // 2
VW = 2 * HD + 1
WIN = 64
HID = 768
HM = HID // 128
ROWS = (128, TOK - 128)
QW = (0, 128)
KW0 = (0, TOK - 2 * 69)
KWN = (128, 138)
UNITS = G * 8
WSCALE = 256.0
INV = 1.0 / WSCALE
MASKED = -61440.0
MASK_ID = 16384.0
LN_EPS = 1e-5


def tile_of(tt):
    half, img = tt // 2, tt % 2
    return half, img, TOK * img + 128 * half, ROWS[half]


def unit_of(u):
    return u // 8, u // 4 % 2, u // 2 % 2, u % 2


def vit_layer(nc, x_t, wp, tok_bias, wqkv, wo, wgu, gate_w, gate_bc, w1, b1, w2, b2, ident, mask_id,
              masks, head_mask, out):
    with ExitStack() as ctx:
        def sb(name, shape, dt=F32):
            return ctx.enter_context(nc.sbuf_tensor(name, shape, dt))

        def sem(name):
            return ctx.enter_context(nc.semaphore(name))

        wp_s = sb("wp_s", [128, 2, PKT, D], F16)
        wqkv_s = sb("wqkv_s", [KB, 2, 3, DB, E * D], F16)
        wgu_s = sb("wgu_s", [KB, 2, G, 2 * D], F16)
        w1_s = sb("w1_s", [KB, 2, DB, E, HID], F16)
        w2_s = sb("w2_s", [128, 2, E, HM, D], F16)
        gate_s = sb("gate_s", [KB, 2, DB, E], F16)
        b2_s = sb("b2_s", [E, 2, D], F16)
        b1_s = sb("b1_s", [128, E, HM])
        tok_bias_s = sb("tok_bias_s", [128, 2, D])
        gate_bc_s = sb("gate_bc_s", [128, 2, E])
        rank_s = sb("rank_s", [128, E])
        ident_s = sb("ident_s", [128, 128])
        mask_id_s = sb("mask_id_s", [128, 128], F16)
        masks_s = sb("masks_s", [128, HU * sum(KWN)], F16)
        head_mask_s = sb("head_mask_s", [KB, HG])

        x_raw = sb("x_raw", [128, PKT, TP])
        x_s = sb("x_s", [128, 2, PKT, TP], F16)
        h = sb("h", [128, 4, D])
        z = sb("z", [128, 4, D])
        zt = sb("zt", [KB, 2, DB, TP], F16)
        stats = sb("stats", [128, 4, 6])
        mv = sb("mv", [128, 4, 2])
        veps = sb("veps", [128, 4])
        rstd = sb("rstd", [128, 4])
        power = sb("power", [128, 4])
        qt_f, kt_f = sb("qt_f", [KB, 2 * G * TP], F16), sb("kt_f", [KB, 2 * G * TP], F16)
        kmask_f = sb("kmask_f", [128, 4 * HG * TP], F16)
        v_f = sb("v_f", [128, PAIR * 3 * E * 12 * VW], F16)
        qt = qt_f[:].rearrange("p (s g t) -> p s g t", s=2, g=G)
        kt = kt_f[:].rearrange("p (s g t) -> p s g t", s=2, g=G)
        kmask = kmask_f[:].rearrange("p (b s h t) -> p b s h t", b=2, s=2, h=HG)
        v = v_f[:].rearrange("p (i n h c) -> p i n h c", i=PAIR, n=3, h=E * 12)
        XR, PR = 4, 3
        p_s = sb("p_s", [128, XR, HU * KWN[1]])
        smax = sb("smax", [128, XR, HU])
        pt = sb("pt", [128, PR, 2, HU * KWN[1]], F16)
        o_raw = sb("o_raw", [128, 2, PAIR, HG, VW])
        o_rcp = sb("o_rcp", [128, 2, PAIR, HG, 1])
        o_g = sb("o_g", [128, 2, 4, HG, HD])
        sig = sb("sig", [128, 4, D])
        up = sb("up", [128, 4, D])
        lg = sb("lg", [128, 4, E])
        top = sb("top", [128, 4, 1])
        onehot = sb("onehot", [128, 4, E])
        onehot_inv = sb("onehot_inv", [128, 4, E])
        oht = sb("oht", [E, TP], F16)
        GR = 3
        gel = sb("gel", [128, GR, TP])
        acc = sb("acc", [128, 4, D])
        ht = kmask_f[:].rearrange("p (b s m t) -> p b s m t", b=2, s=2, m=HM)

        bank = [ctx.enter_context(nc.psum_tensor(f"bank{n}", [128, 512], F32)) for n in range(8)]

        const_in = sem("const_in")
        stage_in = sem("stage_in")
        x_in = sem("x_in")
        y_out = sem("y_out")
        split_hi = sem("split_hi")
        split_lo = sem("split_lo")
        merge_mm = sem("merge_mm")
        x_split = sem("x_split")
        names = """patch_mm var_ready rstd_ready z_ready zt_mm zt_hi zt_lo proj_mm proj_hi proj_lo v_dup k_masked
            scores_mm max_ready shifted p_ready pt_mm pt_hi pt_lo pv_mm o_copied o_summed o_rcp_ready o_ready
            ot_mm ot_hi ot_lo gu_mm sig_ready dve_own
            lg_mm onehot_ready oht_mm oht_ready b2_mm acc_ready hid_mm gel_ready ht_hi ht_lo ffn_mm
            y_ready x_hi x_lo""".split()
        S = {n: sem(n) for n in names}
        nums = sorted(s.num for s in S.values())
        assert nums == list(range(nums[0], nums[0] + len(nums)))
        per_pair = range(nums[0], nums[-1] + 1)

        stage_a = v_f[:].bitcast(F32)
        stage_b = kmask_f[:].bitcast(F32)
        merge_a = qt_f[:].bitcast(F32)
        merge_b = kt_f[:].bitcast(F32)
        wo_raw = merge_a[:, 0:DB * E * D].rearrange("p (k e i) -> p k e i", k=DB, e=E)
        wgu_raw = merge_b[:, 0:G * 2 * D].rearrange("p (g n) -> p g n", g=G)

        def flat(t, part, rows):
            a = t[0:rows, part]
            n = len(a.shape)
            return a if n == 2 else a.rearrange({3: "p a b -> p (a b)", 4: "p a b c -> p (a b c)"}[n])

        half1 = DB * E * HID // 2
        n_qkv, n_w2, n_wp, n_gate = 3 * DB * E * D, E * HM * D, PKT * D, DB * E
        splits = [
            (stage_a, 0, n_qkv, KB, wqkv, lambda s: flat(wqkv_s, s, KB)),
            (stage_b, 0, half1, KB, w1[:, 0:half1], lambda s: flat(w1_s, s, KB)[:, 0:half1]),
            (stage_b, half1, n_wp, 128, wp, lambda s: flat(wp_s, s, 128)),
            (stage_a, 0, n_w2, 128, w2, lambda s: flat(w2_s, s, 128)),
            (stage_b, 0, half1, KB, w1[:, half1:2 * half1], lambda s: flat(w1_s, s, KB)[:, half1:2 * half1]),
            (stage_b, half1, n_gate, KB, gate_w, lambda s: flat(gate_s, s, KB)),
            (stage_b, half1 + n_gate, D, E, b2, lambda s: b2_s[:, s, :]),
        ]
        frees = [0, 0, 0, 1, 3, 3, 3]
        scale_of = [WSCALE] * 6 + [1.0]

        with nc.Block() as block:
            @block.sync
            def _(sp):
                sp.dma_start(x_raw[:], x_t[0]).then_inc(x_in, 16)
                consts = [(ident_s, ident), (mask_id_s, mask_id), (masks_s, masks), (head_mask_s, head_mask),
                          (tok_bias_s, tok_bias), (b1_s, b1)]
                for dst, src in consts:
                    sp.dma_start(dst[:], src).then_inc(const_in, 16)
                sp.dma_start(gate_bc_s[:], gate_bc).then_inc(y_out, 16)
                sp.dma_start(wo_raw, wo).then_inc(const_in, 16)
                sp.dma_start(wgu_raw, wgu).then_inc(const_in, 16)
                for n, (stage, c0, cols, rows, src, _) in enumerate(splits):
                    if frees[n]:
                        sp.wait_ge(split_lo, frees[n])
                    sp.dma_start(stage[0:rows, c0:c0 + cols], src).then_inc(stage_in, 16)
                    sp.wait_ge(stage_in, 16 * (n + 1))

            @block.scalar
            def _(act):
                for n, (stage, c0, cols, rows, _, target) in enumerate(splits):
                    act.wait_ge(stage_in, 16 * (n + 1))
                    nc.scalar.activation(target(0), stage[0:rows, c0:c0 + cols], ACT.Copy,
                                         scale=scale_of[n]).then_inc(split_hi, 1)
                for g in range(G):
                    act.wait_ge(merge_mm, g + 1)
                    nc.scalar.activation(wgu_s[:, 0, g, :], bank[g][0:KB, 0:2 * D], ACT.Copy,
                                         scale=WSCALE).then_inc(split_hi, 1)
                act.wait_ge(x_in, 16)
                nc.scalar.copy(x_s[:, 0], x_raw[:]).then_inc(split_hi, 1)

            @block.vector
            def _(dve):
                for n, (stage, c0, cols, rows, _, target) in enumerate(splits):
                    dve.wait_ge(split_hi, n + 1)
                    nc.vector.scalar_tensor_tensor(out=target(1), in0=stage[0:rows, c0:c0 + cols],
                                                   scalar=scale_of[n], in1=target(0), op0=ALU.mult,
                                                   op1=ALU.subtract).then_inc(split_lo, 1)
                for g in range(G):
                    dve.wait_ge(split_hi, len(splits) + g + 1)
                    nc.vector.scalar_tensor_tensor(out=wgu_s[:, 1, g, :], in0=bank[g][0:KB, 0:2 * D],
                                                   scalar=WSCALE, in1=wgu_s[:, 0, g, :], op0=ALU.mult,
                                                   op1=ALU.subtract).then_inc(split_lo, 1)
                dve.wait_ge(split_hi, len(splits) + G + 1)
                nc.vector.tensor_tensor(x_s[:, 1], x_raw[:], x_s[:, 0], ALU.subtract).then_inc(split_lo, 1)
                dve.wait_ge(split_lo, 4)
                nc.vector.memset(v[:, :, :, :, 2 * HD:VW], 1.0)
                nc.vector.memset(power[:], -0.5)
                for e in range(E):
                    nc.vector.memset(rank_s[:, e:e + 1], float(E - e))

            @block.tensor
            def _(pe):
                pe.wait_ge(const_in, 16 * 8)
                for g in range(G):
                    e, i0 = g // DB, g % DB * KB
                    for k in range(DB):
                        mm = nc.tensor.matmul(bank[g][0:KB, 0:2 * D], wo_raw[:, k, e, i0:i0 + KB],
                                              wgu_raw[:, e * DB + k, :], start=(k == 0), stop=(k == DB - 1))
                    mm.then_inc(merge_mm, 1)

        proj = [("k", 0), ("q", 0)] + [("v", n) for n in range(8)]
        for g in range(1, G):
            proj += [("k", g), ("q", g)]
        v_first = 2

        def proj_psum(n):
            kind, j = proj[n]
            if kind == "v":
                return bank[n % 8][0:ROWS[j // 4], 0:2 * D]
            return bank[n % 8][0:KB, 0:TP]

        def proj_target(n, part):
            kind, j = proj[n]
            if kind == "v":
                half, img, _, rows = tile_of(j // 2)
                return v[0:rows, img, 2 * half, 24 * (j % 2):24 * (j % 2) + 24, part * HD:part * HD + HD]
            return (kt if kind == "k" else qt)[:, part, j, :]

        def proj_src(n):
            p = proj_psum(n)
            return p.rearrange("p (h d) -> p h d", d=HD) if proj[n][0] == "v" else p

        def three(pairs):
            return [(a(s), b(m)) for a, b in pairs for s, m in ((0, 0), (0, 1), (1, 0))]

        def product(psum, pairs):
            passes = three(pairs)
            for n, (stat, mov) in enumerate(passes):
                mm = nc.tensor.matmul(psum, stat, mov, start=(n == 0), stop=(n == len(passes) - 1))
            return mm

        def o_bank(w):
            return bank[6 + w % 2][:, 0:PAIR * HG * VW].rearrange("p (i h c) -> p i h c", i=PAIR, h=HG)

        def k_first(g):
            return 2 * HG * (g + 1)

        LAG_T, LAG_PV = 3, 4
        LAG_OC, LAG_OR, LAG_OT, LAG_OTE = 5, 6, 8, 9
        PIPE = UNITS + LAG_OTE + 1

        def window_at(s, lag):
            u = s - lag
            return u // 4 if 0 <= u < UNITS and u % 4 == 3 else None

        with nc.Fori(0, STEPS) as i:
            with nc.Block(no_gpsimd_drain=True) as block:

                @block.sync
                def _(sp):
                    sp.dma_start(x_raw[:], x_t[(i + 1) % STEPS]).then_inc(x_in, 16)
                    for img in range(PAIR):
                        sp.wait_ge(S["proj_lo"], v_first + 2 * img + 2)
                        sp.dma_start(v[0:69, img, 1], v[KW0[1]:128, img, 0]).then_inc(S["v_dup"], 16)
                    for tt in range(4):
                        half, img, _, rows = tile_of(tt)
                        sp.wait_ge(S["y_ready"], tt + 1)
                        sp.dma_start(out[i, img, 128 * half:128 * half + rows, :],
                                     acc[0:rows, tt, :]).then_inc(y_out, 16)

                @block.tensor
                def _(pe):
                    for tt in range(4):
                        _, _, c0, rows = tile_of(tt)
                        product(bank[tt][0:rows, 0:D],
                                [(lambda s, k=k: x_s[:, s, k, c0:c0 + rows], lambda s, k=k: wp_s[:, s, k, :])
                                 for k in range(PKT)]).then_inc(S["patch_mm"], 1)

                    def turn_z(times):
                        for tt in range(4):
                            _, _, c0, rows = tile_of(tt)
                            pe.wait_ge(S["z_ready"], 4 * times + tt + 1)
                            for k in range(DB):
                                mm = nc.tensor.transpose(bank[4 + k][0:KB, c0:c0 + rows],
                                                         z[0:rows, tt, KB * k:KB * k + KB],
                                                         ident_s[0:rows, 0:rows])
                        mm.then_inc(S["zt_mm"], 1)

                    turn_z(0)
                    pe.wait_ge(S["zt_lo"], 2)
                    for n, (kind, j) in enumerate(proj):
                        if n >= 8:
                            pe.wait_ge(S["proj_lo"], n - 7)
                        if kind == "v":
                            _, _, c0, rows = tile_of(j // 2)
                            w0 = 2 * D * (j % 2)
                            ops = [(lambda s, k=k: zt[:, s, k, c0:c0 + rows],
                                    lambda s, k=k: wqkv_s[:, s, 2, k, w0:w0 + 2 * D]) for k in range(DB)]
                        else:
                            m = 0 if kind == "q" else 1
                            ops = [(lambda s, k=k: wqkv_s[:, s, m, k, KB * j:KB * j + KB],
                                    lambda s, k=k: zt[:, s, k, :]) for k in range(DB)]
                        product(proj_psum(n), ops).then_inc(S["proj_mm"], 1)

                    def scores(u):
                        g, half, hh, img = unit_of(u)
                        q0, rows = TOK * img + QW[half], ROWS[half]
                        k0, kn = TOK * img + KW0[half], KWN[half]
                        if u % 8 == 0:
                            pe.wait_ge(S["k_masked"], k_first(g))
                        if u >= 3:
                            pe.wait_ge(S["shifted"], u - 2)
                        ps = bank[u % 3][0:rows, 0:HU * kn]
                        for n, (s, m) in enumerate(((0, 0), (0, 1), (1, 0))):
                            nc.tensor.matmul(ps, qt[:, s, g, q0:q0 + rows],
                                             kmask[0:KB, g % 2, m, HU * hh:HU * hh + HU, k0:k0 + kn],
                                             start=(n == 0), stop=False)
                        m0 = half * HU * KWN[0]
                        nc.tensor.matmul(ps, mask_id_s[0:rows, 0:rows], masks_s[0:rows, m0:m0 + HU * kn],
                                         start=False, stop=True).then_inc(S["scores_mm"], 1)

                    def turn_p(u):
                        _, half, _, _ = unit_of(u)
                        rows, kn, nk = ROWS[half], KWN[half], (128, 69)[half]
                        pe.wait_ge(S["p_ready"], u + 1)
                        if u >= 2:
                            pe.wait_ge(S["pt_lo"], u - 1)
                        for b in range(HU * kn // nk):
                            mm = nc.tensor.transpose(bank[3 + u % 2][0:nk, b * nk:b * nk + nk][:, 0:rows],
                                                     p_s[0:rows, u % XR, b * nk:b * nk + nk],
                                                     ident_s[0:rows, 0:rows])
                        mm.then_inc(S["pt_mm"], 1)

                    def times_v(u):
                        g, half, hh, img = unit_of(u)
                        w = u // 4
                        rows, nk = ROWS[half], (128, 69)[half]
                        pe.wait_ge(S["pt_lo"], u + 1)
                        if u == 0:
                            pe.wait_ge(S["proj_lo"], v_first + 8)
                        if u == 4:
                            pe.wait_ge(S["v_dup"], 32)
                        if u % 4 == 0 and w >= 2:
                            pe.wait_ge(S["o_copied"], w - 1)
                        for j in range(HU):
                            head = HG * g + HU * hh + j
                            parts = [(b, s) for b in range(1 + half) for s in range(2)]
                            for n, (b, s) in enumerate(parts):
                                c = ((1 + half) * j + b) * nk
                                mm = nc.tensor.matmul(o_bank(w)[0:rows, img, HU * hh + j, :],
                                                      pt[0:nk, u % PR, s, c:c + rows],
                                                      v[0:nk, img, half + b, head, :],
                                                      start=(n == 0), stop=(n == len(parts) - 1))
                        mm.then_inc(S["pv_mm"], 1)

                    def turn_o(g):
                        pe.wait_ge(S["o_ready"], 2 * g + 2)
                        if g >= 1:
                            pe.wait_ge(S["ot_lo"], g)
                        for tt in range(4):
                            _, _, c0, rows = tile_of(tt)
                            mm = nc.tensor.transpose(bank[5][0:KB, c0:c0 + rows],
                                                     o_g[0:rows, g % 2, tt].rearrange("p h d -> p (h d)"),
                                                     ident_s[0:rows, 0:rows])
                        mm.then_inc(S["ot_mm"], 1)

                    pe.wait_ge(S["proj_lo"], len(proj))
                    for s in range(PIPE):
                        if s < UNITS:
                            scores(s)
                        if 0 <= s - LAG_T < UNITS:
                            turn_p(s - LAG_T)
                        if 0 <= s - LAG_PV < UNITS:
                            times_v(s - LAG_PV)
                        w = window_at(s, LAG_OT)
                        if w is not None and w % 2 == 1:
                            turn_o(w // 2)

                    pe.wait_ge(S["ot_lo"], G)
                    for tt in range(4):
                        _, _, c0, rows = tile_of(tt)
                        product(bank[tt][0:rows, 0:2 * D],
                                [(lambda s, g=g: qt[:, s, g, c0:c0 + rows], lambda s, g=g: wgu_s[:, s, g, :])
                                 for g in range(G)]).then_inc(S["gu_mm"], 1)

                    turn_z(1)
                    pe.wait_ge(S["zt_lo"], 4)
                    for tt in range(4):
                        _, _, c0, rows = tile_of(tt)
                        mm = product(bank[6][0:rows, E * tt:E * tt + E],
                                     [(lambda s, k=k: zt[:, s, k, c0:c0 + rows],
                                       lambda s, k=k: gate_s[:, s, k, :]) for k in range(DB)])
                    mm.then_inc(S["lg_mm"], 1)

                    def hidden(e):
                        for m in range(HM):
                            a = HM * e + m
                            if a >= 4:
                                pe.wait_ge(S["gel_ready"], a - 3)
                            product(bank[a % 4][:, 0:TP],
                                    [(lambda s, k=k: w1_s[:, s, k, e, 128 * m:128 * m + 128],
                                      lambda s, k=k: zt[:, s, k, :]) for k in range(DB)]
                                    ).then_inc(S["hid_mm"], 1)

                    def expert_out(e):
                        pe.wait_ge(S["ht_lo"], HM * (e + 1))
                        for tt in range(4):
                            _, _, c0, rows = tile_of(tt)
                            b = 4 * e + tt
                            if b >= 2:
                                pe.wait_ge(S["acc_ready"], 2 + b - 1)
                            product(bank[4 + b % 2][0:rows, 0:D],
                                    [(lambda s, m=m: ht[:, e % 2, s, m, c0:c0 + rows],
                                      lambda s, m=m: w2_s[:, s, e, m, :]) for m in range(HM)]
                                    ).then_inc(S["ffn_mm"], 1)

                    hidden(0)
                    pe.wait_ge(S["onehot_ready"], 2)
                    for tt in range(4):
                        _, _, c0, rows = tile_of(tt)
                        mm = nc.tensor.transpose(bank[7][0:E, c0:c0 + rows], onehot[0:rows, tt, :],
                                                 ident_s[0:rows, 0:rows])
                    mm.then_inc(S["oht_mm"], 1)
                    hidden(1)
                    pe.wait_ge(S["oht_ready"], 1)
                    for tt in range(4):
                        half, img, c0, rows = tile_of(tt)
                        for s in range(2):
                            mm = nc.tensor.matmul(bank[6 + half][0:rows, D * img:D * img + D],
                                                  oht[:, c0:c0 + rows], b2_s[:, s, :],
                                                  start=(s == 0), stop=(s == 1))
                        if img == 1:
                            mm.then_inc(S["b2_mm"], 1)
                    expert_out(0)
                    hidden(2)
                    expert_out(1)
                    hidden(3)
                    expert_out(2)
                    expert_out(3)

                @block.scalar
                def _(act):
                    def zt_high(times):
                        act.wait_ge(S["zt_mm"], times + 1)
                        for k in range(DB):
                            nc.scalar.copy(zt[:, 0, k, :], bank[4 + k][0:KB, 0:TP]).then_inc(S["zt_hi"], 1)

                    zt_high(0)
                    for n in range(len(proj)):
                        act.wait_ge(S["proj_mm"], n + 1)
                        nc.scalar.activation(proj_target(n, 0), proj_src(n), ACT.Copy,
                                             scale=INV).then_inc(S["proj_hi"], 1)
                    for s in range(PIPE):
                        u = s - 1
                        if 0 <= u < UNITS:
                            half = unit_of(u)[1]
                            act.wait_ge(S["shifted"], u + 1)
                            pu = p_s[0:ROWS[half], u % XR, 0:HU * KWN[half]]
                            nc.scalar.activation(pu, pu, ACT.Exp, scale=HD ** -0.5).then_inc(S["p_ready"], 1)
                        u = s - LAG_T
                        if 0 <= u < UNITS:
                            half = unit_of(u)[1]
                            nk, n = (128, 69)[half], HU * KWN[half]
                            act.wait_ge(S["pt_mm"], u + 1)
                            if u >= PR:
                                act.wait_ge(S["pv_mm"], u - PR + 1)
                            nc.scalar.copy(pt[0:nk, u % PR, 0, 0:n], bank[3 + u % 2][0:nk, 0:n]
                                           ).then_inc(S["pt_hi"], 1)
                        w = window_at(s, LAG_OC)
                        if w is not None:
                            rows = ROWS[w % 2]
                            act.wait_ge(S["pv_mm"], 4 * w + 4)
                            if w >= 2:
                                act.wait_ge(S["o_ready"], w - 1)
                            nc.scalar.copy(o_raw[0:rows, w % 2], o_bank(w)[0:rows]).then_inc(S["o_copied"], 1)
                        w = window_at(s, LAG_OTE)
                        if w is not None and w % 2 == 1:
                            g = w // 2
                            act.wait_ge(S["ot_mm"], g + 1)
                            nc.scalar.copy(qt[:, 0, g, :], bank[5][0:KB, 0:TP]).then_inc(S["ot_hi"], 1)
                    for tt in range(4):
                        rows = tile_of(tt)[3]
                        act.wait_ge(S["gu_mm"], tt + 1)
                        nc.scalar.activation(sig[0:rows, tt, :], bank[tt][0:rows, 0:D], ACT.Exp,
                                             scale=-INV).then_inc(S["sig_ready"], 1)
                    zt_high(1)
                    for a in range(E * HM):
                        e, m = a // HM, a % HM
                        act.wait_ge(S["hid_mm"], a + 1)
                        if a >= GR:
                            act.wait_ge(S["ht_lo"], a - GR + 1)
                        nc.scalar.activation(gel[:, a % GR, :], bank[a % 4][:, 0:TP], ACT.Gelu,
                                             bias=b1_s[:, e, m:m + 1], scale=INV).then_inc(S["gel_ready"], 1)
                    act.wait_ge(x_in, 16 * i + 32)
                    nc.scalar.copy(x_s[:, 0], x_raw[:]).then_inc(S["x_hi"], 1)

                @block.gpsimd
                def _(pool):
                    def inverse_std(times):
                        for half in range(2):
                            t0, rows = 2 * half, ROWS[half]
                            pool.wait_ge(S["var_ready"], 2 * times + half + 1)
                            nc.gpsimd.tensor_tensor(rstd[0:rows, t0:t0 + 2], veps[0:rows, t0:t0 + 2],
                                                    power[0:rows, t0:t0 + 2], ALU.pow).then_inc(S["rstd_ready"], 1)

                    inverse_std(0)
                    for w in range(2 * G):
                        half, g = w % 2, w // 2
                        rows = ROWS[half]
                        o = o_g[0:rows, g % 2, 2 * half:2 * half + 2]
                        pool.wait_ge(S["o_copied"], w + 1)
                        if w >= 4:
                            pool.wait_ge(S["ot_mm"], g - 1)
                        nc.gpsimd.tensor_tensor(o, o_raw[0:rows, w % 2, :, :, 0:HD],
                                                o_raw[0:rows, w % 2, :, :, HD:2 * HD],
                                                ALU.add).then_inc(S["o_summed"], 1)
                        pool.wait_ge(S["o_summed"], w + 1)
                        pool.wait_ge(S["o_rcp_ready"], w + 1)
                        nc.gpsimd.tensor_tensor(o, o, o_rcp[0:rows, w % 2].broadcast_to([rows, PAIR, HG, HD]),
                                                ALU.mult).then_inc(S["o_ready"], 1)
                    inverse_std(1)
                    pool.wait_ge(S["x_hi"], 1)
                    nc.gpsimd.tensor_tensor(x_s[:, 1], x_raw[:], x_s[:, 0], ALU.subtract).then_inc(S["x_lo"], 1)

                @block.vector
                def _(dve):
                    own = [0]

                    def chain(ins):
                        own[0] += 1
                        ins.then_inc(S["dve_own"], 1)
                        dve.wait_ge(S["dve_own"], own[0])

                    def moments(tt):
                        half, img, _, rows = tile_of(tt)
                        chain(nc.vector.bn_stats(stats[0:rows, tt, :], h[0:rows, tt, :]))
                        chain(nc.vector.bn_aggr(mv[0:rows, tt, :], stats[0:rows, tt, :]))
                        if img == 1:
                            nc.vector.tensor_scalar(veps[0:rows, 2 * half:2 * half + 2], mv[0:rows, tt - 1:tt + 1, 1],
                                                    LN_EPS, None, ALU.add).then_inc(S["var_ready"], 1)

                    def normalise(times, tt):
                        half, img, _, rows = tile_of(tt)
                        dve.wait_ge(S["rstd_ready"], 2 * times + half + 1)
                        nc.vector.tensor_scalar(z[0:rows, tt, :], h[0:rows, tt, :], mv[0:rows, tt, 0:1],
                                                rstd[0:rows, tt:tt + 1], ALU.subtract,
                                                ALU.mult).then_inc(S["z_ready"], 1)

                    def zt_low(times):
                        for k in range(DB):
                            dve.wait_ge(S["zt_hi"], DB * times + k + 1)
                            nc.vector.tensor_tensor(zt[:, 1, k, :], bank[4 + k][0:KB, 0:TP], zt[:, 0, k, :],
                                                    ALU.subtract).then_inc(S["zt_lo"], 1)

                    for tt in range(4):
                        half, _, _, rows = tile_of(tt)
                        dve.wait_ge(S["patch_mm"], tt + 1)
                        chain(nc.vector.scalar_tensor_tensor(out=h[0:rows, tt, :], in0=bank[tt][0:rows, 0:D],
                                                             scalar=INV, in1=tok_bias_s[0:rows, half, :],
                                                             op0=ALU.mult, op1=ALU.add))
                        moments(tt)
                    for tt in range(4):
                        normalise(0, tt)
                    zt_low(0)

                    def mask_keys(n):
                        g, s, j = n // (2 * HG), n // HG % 2, n % HG
                        nc.vector.tensor_scalar(kmask[0:KB, g % 2, s, j, :], kt[:, s, g, :],
                                                head_mask_s[:, j:j + 1], None, ALU.mult
                                                ).then_inc(S["k_masked"], 1)

                    for n in range(len(proj)):
                        dve.wait_ge(S["proj_hi"], n + 1)
                        nc.vector.scalar_tensor_tensor(out=proj_target(n, 1), in0=proj_src(n), scalar=INV,
                                                       in1=proj_target(n, 0), op0=ALU.mult,
                                                       op1=ALU.subtract).then_inc(S["proj_lo"], 1)
                        if n == 10:
                            dve.wait_ge(S["proj_lo"], 1)
                            for m in range(2 * HG):
                                mask_keys(m)

                    dve.wait_ge(S["proj_lo"], len(proj))
                    masked = 2 * HG
                    for s in range(PIPE):
                        if s < UNITS:
                            half = unit_of(s)[1]
                            rows, kn = ROWS[half], KWN[half]
                            dve.wait_ge(S["scores_mm"], s + 1)
                            nc.vector.reduce_max(smax[0:rows, s % XR, :], bank[s % 3][0:rows, 0:HU * kn].rearrange(
                                "p (h k) -> p h k", h=HU), AX_X).then_inc(S["max_ready"], 1)
                        g = s // 8 + 1
                        if g < G and s % 8 < HG:
                            if g >= 2:
                                dve.wait_ge(S["scores_mm"], 8 * (g - 1))
                            mask_keys(masked)
                            mask_keys(masked + 1)
                            masked += 2
                        u = s - 1
                        if 0 <= u < UNITS:
                            half = unit_of(u)[1]
                            rows, kn = ROWS[half], KWN[half]
                            dve.wait_ge(S["max_ready"], u + 1)
                            if u >= XR:
                                dve.wait_ge(S["pt_mm"], u - XR + 1)
                            nc.vector.tensor_tensor(
                                p_s[0:rows, u % XR, 0:HU * kn].rearrange("p (h k) -> p h k", h=HU),
                                bank[u % 3][0:rows, 0:HU * kn].rearrange("p (h k) -> p h k", h=HU),
                                smax[0:rows, u % XR, :].unsqueeze(2).broadcast_to([rows, HU, kn]),
                                ALU.subtract).then_inc(S["shifted"], 1)
                        u = s - LAG_T
                        if 0 <= u < UNITS:
                            half = unit_of(u)[1]
                            nk, n = (128, 69)[half], HU * KWN[half]
                            dve.wait_ge(S["pt_hi"], u + 1)
                            nc.vector.tensor_tensor(pt[0:nk, u % PR, 1, 0:n], bank[3 + u % 2][0:nk, 0:n],
                                                    pt[0:nk, u % PR, 0, 0:n], ALU.subtract
                                                    ).then_inc(S["pt_lo"], 1)
                        w = window_at(s, LAG_OR)
                        if w is not None:
                            rows = ROWS[w % 2]
                            dve.wait_ge(S["o_copied"], w + 1)
                            if w >= 2:
                                dve.wait_ge(S["o_ready"], w - 1)
                            nc.vector.reciprocal(o_rcp[0:rows, w % 2], o_raw[0:rows, w % 2, :, :, 2 * HD:VW]
                                                 ).then_inc(S["o_rcp_ready"], 1)
                        w = window_at(s, LAG_OTE)
                        if w is not None and w % 2 == 1:
                            g = w // 2
                            dve.wait_ge(S["ot_hi"], g + 1)
                            nc.vector.tensor_tensor(qt[:, 1, g, :], bank[5][0:KB, 0:TP], qt[:, 0, g, :],
                                                    ALU.subtract).then_inc(S["ot_lo"], 1)

                    for tt in range(4):
                        rows = tile_of(tt)[3]
                        sg, upt = sig[0:rows, tt, :], up[0:rows, tt, :]
                        dve.wait_ge(S["sig_ready"], tt + 1)
                        chain(nc.vector.tensor_scalar(sg, sg, 1.0, None, ALU.add))
                        chain(nc.vector.reciprocal(sg, sg))
                        chain(nc.vector.scalar_tensor_tensor(out=upt, in0=bank[tt][0:rows, 0:D], scalar=INV, in1=sg,
                                                             op0=ALU.mult, op1=ALU.mult))
                        chain(nc.vector.scalar_tensor_tensor(out=upt, in0=bank[tt][0:rows, D:2 * D], scalar=INV,
                                                             in1=upt, op0=ALU.mult, op1=ALU.mult))
                        chain(nc.vector.tensor_tensor(h[0:rows, tt, :], h[0:rows, tt, :], upt, ALU.add))
                        moments(tt)
                    for tt in range(4):
                        normalise(1, tt)
                    zt_low(1)

                    dve.wait_ge(S["lg_mm"], 1)
                    for half in range(2):
                        rows, t0 = ROWS[half], 2 * half
                        lgh, toph = lg[0:rows, t0:t0 + 2, :], top[0:rows, t0:t0 + 2, :]
                        oh = onehot[0:rows, t0:t0 + 2, :]
                        wide = [rows, 2, E]
                        chain(nc.vector.scalar_tensor_tensor(
                            out=lgh, in0=bank[6][0:rows, E * t0:E * t0 + 2 * E].rearrange("p (t e) -> p t e", e=E),
                            scalar=INV, in1=gate_bc_s[0:rows, 0:1, :].broadcast_to(wide), op0=ALU.mult,
                            op1=ALU.add))
                        chain(nc.vector.tensor_tensor(lgh, lgh, gate_bc_s[0:rows, 1:2, :].broadcast_to(wide),
                                                      ALU.subtract))
                        chain(nc.vector.reduce_max(toph, lgh, AX_X))
                        chain(nc.vector.tensor_tensor(oh, lgh, toph.broadcast_to(wide), ALU.is_ge))
                        chain(nc.vector.tensor_tensor(oh, oh, rank_s[0:rows, :].unsqueeze(1).broadcast_to(wide),
                                                      ALU.mult))
                        chain(nc.vector.reduce_max(toph, oh, AX_X))
                        chain(nc.vector.tensor_tensor(oh, oh, toph.broadcast_to(wide), ALU.is_ge))
                        nc.vector.tensor_scalar(onehot_inv[0:rows, t0:t0 + 2, :], oh, INV, None,
                                                ALU.mult).then_inc(S["onehot_ready"], 1)

                    def split_hidden(e):
                        for m in range(HM):
                            a = HM * e + m
                            dve.wait_ge(S["gel_ready"], a + 1)
                            if e >= 2 and m == 0:
                                dve.wait_ge(S["ffn_mm"], 4 * (e - 1))
                            nc.vector.tensor_copy(ht[:, e % 2, 0, m, :], gel[:, a % GR, :]).then_inc(S["ht_hi"], 1)
                            dve.wait_ge(S["ht_hi"], a + 1)
                            nc.vector.tensor_tensor(ht[:, e % 2, 1, m, :], gel[:, a % GR, :], ht[:, e % 2, 0, m, :],
                                                    ALU.subtract).then_inc(S["ht_lo"], 1)

                    def add_expert(e):
                        for tt in range(4):
                            rows = tile_of(tt)[3]
                            b = 4 * e + tt
                            dve.wait_ge(S["ffn_mm"], b + 1)
                            dve.wait_ge(S["acc_ready"], 2 + b)
                            ins = nc.vector.scalar_tensor_tensor(
                                out=acc[0:rows, tt, :], in0=bank[4 + b % 2][0:rows, 0:D],
                                scalar=onehot_inv[0:rows, tt, e:e + 1], in1=acc[0:rows, tt, :], op0=ALU.mult,
                                op1=ALU.add)
                            ins.then_inc(S["acc_ready"], 1)
                            if e == E - 1:
                                dve.wait_ge(S["acc_ready"], 2 + b + 1)
                                dve.engine_nop().then_inc(S["y_ready"], 1)

                    split_hidden(0)
                    dve.wait_ge(S["oht_mm"], 1)
                    nc.vector.tensor_copy(oht[:], bank[7][0:E, 0:TP]).then_inc(S["oht_ready"], 1)
                    split_hidden(1)
                    dve.wait_ge(y_out, 64 * i + 16)
                    for half in range(2):
                        rows, t0 = ROWS[half], 2 * half
                        dve.wait_ge(S["b2_mm"], half + 1)
                        nc.vector.tensor_tensor(acc[0:rows, t0:t0 + 2, :], h[0:rows, t0:t0 + 2, :],
                                                bank[6 + half][0:rows, 0:2 * D].rearrange("p (t d) -> p t d", t=2),
                                                ALU.add).then_inc(S["acc_ready"], 1)
                    add_expert(0)
                    split_hidden(2)
                    add_expert(1)
                    split_hidden(3)
                    add_expert(2)
                    add_expert(3)

            nc.all_engine_barrier(sems_to_clear=per_pair)

        with nc.Block() as block:
            @block.sync
            def _(sp):
                sp.wait_ge(y_out, 64 * STEPS + 16)


def layouts(x, cls_tok, L0_tok_W_proj, L0_tok_b_proj, L0_attn_wq, L0_attn_wk, L0_attn_wv, L0_attn_wo,
            L0_attn_w_gate, L0_attn_w_up, L0_ffn_gate_w, L0_ffn_gate_b, L0_ffn_gate_center, L0_ffn_w1,
            L0_ffn_b1, L0_ffn_w2, L0_ffn_b2):
    import numpy as np
    f = np.float32

    def rows(a, kb):
        return a.reshape(-1, kb, *a.shape[1:]).swapaxes(0, 1)

    p = x.reshape(IMGS, 3, 14, 16, 14, 16).transpose(1, 3, 5, 0, 2, 4).reshape(PATCH, STEPS, PAIR, TOK - 1)
    x_t = np.zeros((STEPS, 128, PKT, PAIR, TOK), f)
    x_t[..., 1:] = p.reshape(PKT, 128, STEPS, PAIR, TOK - 1).transpose(2, 1, 0, 3, 4)
    tok_bias = np.empty((128, 2, D), f)
    tok_bias[:] = L0_tok_b_proj
    tok_bias[0, 0] = cls_tok[0, 0]
    gate_bc = np.empty((128, 2, E), f)
    gate_bc[:, 0] = L0_ffn_gate_b
    gate_bc[:, 1] = L0_ffn_gate_center
    wqkv = np.stack([rows(w.transpose(2, 0, 1).reshape(D, E * D), KB)
                     for w in (L0_attn_wq, L0_attn_wk, L0_attn_wv)], 1)
    wgu = np.concatenate([L0_attn_w_gate.T, L0_attn_w_up.T], 1)
    masks = []
    for half in range(2):
        q = QW[half] + np.arange(128)[:, None]
        k = KW0[half] + np.arange(KWN[half])[None, :]
        m = np.where((q - k >= 0) & (q - k < WIN), 0.0, MASKED)
        masks.append(np.tile(m, (1, HU)))
    c = np.ascontiguousarray
    return dict(
        x_t=x_t.reshape(STEPS, 128, PKT, TP),
        wp=c(rows(L0_tok_W_proj.T, 128).reshape(128, -1)),
        tok_bias=tok_bias,
        wqkv=c(wqkv.reshape(KB, -1)),
        wo=c(rows(L0_attn_wo.transpose(1, 0, 2), KB)),
        wgu=c(rows(wgu, KB)),
        gate_w=c(rows(L0_ffn_gate_w, KB).reshape(KB, -1)),
        gate_bc=gate_bc,
        w1=c(rows(L0_ffn_w1.transpose(1, 0, 2), KB).reshape(KB, -1)),
        b1=c(L0_ffn_b1.reshape(E, HM, 128).transpose(2, 0, 1)),
        w2=c(L0_ffn_w2.reshape(E, HM, 128, D).transpose(2, 0, 1, 3).reshape(128, -1)),
        b2=c(L0_ffn_b2),
        ident=np.eye(128, dtype=f),
        mask_id=(MASK_ID * np.eye(128)).astype(np.float16),
        masks=np.concatenate(masks, 1).astype(np.float16),
        head_mask=np.kron(np.eye(HG), np.ones((HD, 1))).astype(f),
    )


def kernel(**inputs):
    import numpy as np
    from concourse import bacc
    from concourse.bass_utils import run_bass_kernel_spmd

    arrays = layouts(**{k: np.asarray(a) for k, a in inputs.items()})
    nc = bacc.Bacc("TRN2", target_bir_lowering=False, num_devices=1)
    args = {n: nc.dram_tensor(f"{n}_dram", a.shape, mybir.dt.from_np(a.dtype), kind="ExternalInput").ap()
            for n, a in arrays.items()}
    out = nc.dram_tensor("out_dram", (STEPS, PAIR, TOK, D), F32, kind="ExternalOutput").ap()
    vit_layer(nc, **args, out=out)
    r = run_bass_kernel_spmd(nc, [{f"{n}_dram": a for n, a in arrays.items()}], core_ids=[0])
    return r.results[0]["out_dram"].reshape(IMGS, TOK, D)
```

```python
from contextlib import ExitStack

import concourse.bass as bass
from concourse import mybir

F32 = mybir.dt.float32
F16 = mybir.dt.float16
ALU = mybir.AluOpType
ACT = mybir.ActivationFunctionType
AX_X = mybir.AxisListType.X

IMGS = 64
PAIR = 2
STEPS = IMGS // PAIR
TOK = 197
TP = PAIR * TOK
D = 192
KB = 96
DB = D // KB
PATCH = 768
PKT = PATCH // 128
E = 4
HD = 16
G = E * D // KB
HG = KB // HD
HU = HG // 2
VW = 2 * HD + 1
WIN = 64
HID = 768
HM = HID // 128
ROWS = (128, TOK - 128)
QW = (0, 128)
KW0 = (0, TOK - 2 * 69)
KWN = (128, 138)
UNITS = G * 8
WSCALE = 256.0
INV = 1.0 / WSCALE
DVE_SHIFTS = (3,)
MASKED = 61440.0
MASK_ID = 16384.0
LN_EPS = 1e-5


def tile_of(tt):
    half, img = tt // 2, tt % 2
    return half, img, TOK * img + 128 * half, ROWS[half]


def unit_of(u):
    return u // 8, u // 4 % 2, u // 2 % 2, u % 2


def vit_layer(nc, x_t, wp, tok_bias, wqkv, wo, wgu, gate_w, gate_bc, w1, b1, w2, b2, ident, mask_id,
              masks, head_mask, out):
    with ExitStack() as ctx:
        def sb(name, shape, dt=F32):
            return ctx.enter_context(nc.sbuf_tensor(name, shape, dt))

        def sem(name):
            return ctx.enter_context(nc.semaphore(name))

        wp_s = sb("wp_s", [128, 2, PKT, D], F16)
        wqkv_s = sb("wqkv_s", [128, 2, 3, 2, E * D], F16)
        wgu_s = sb("wgu_s", [128, 2, 2 * E, 2 * D], F16)
        w1_s = sb("w1_s", [128, 2, 2, E, HID], F16)
        w2_s = sb("w2_s", [128, 2, E, HM, D], F16)
        gate_s = sb("gate_s", [128, 2, 2, E], F16)
        b2_s = sb("b2_s", [E, 2, D], F16)
        b1_s = sb("b1_s", [128, E, HM])
        tok_bias_s = sb("tok_bias_s", [128, 2, D])
        gate_bc_s = sb("gate_bc_s", [128, 2, E])
        rank_s = sb("rank_s", [128, E])
        ident_s = sb("ident_s", [128, 128])
        mask_id_s = sb("mask_id_s", [128, 128], F16)
        masks_s = sb("masks_s", [128, HU * sum(KWN)], F16)
        head_mask_s = sb("head_mask_s", [KB, HG], F16)

        x_s = sb("x_s", [128, 2, PKT, TP], F16)
        h_next = sb("h_next", [128, 4, D])
        h = sb("h", [128, 4, D])
        z = sb("z", [128, 4, 256])
        zt1 = sb("zt1", [128, 3, TP], F16)
        zt2 = sb("zt2", [128, 3, TP], F16)
        stats = sb("stats", [128, 4, 6])
        mv = sb("mv", [128, 4, 2])
        veps = sb("veps", [128, 4])
        rstd = sb("rstd", [128, 4])
        power = sb("power", [128, 4])
        qt_f, kt_f = sb("qt_f", [128, 2 * G * TP], F16), sb("kt_f", [128, 2 * G * TP], F16)
        kmask_f = sb("kmask_f", [128, 4 * HG * TP], F16)
        v_f = sb("v_f", [128, PAIR * 3 * E * 12 * VW], F16)
        qt = qt_f[0:KB].rearrange("p (g s t) -> p g s t", s=2, g=G)
        kt = kt_f[0:KB].rearrange("p (g s t) -> p g s t", s=2, g=G)
        ot = qt_f[:].rearrange("p (e c t) -> p e c t", e=E, c=4)
        kmask = kmask_f[:].rearrange("p (b s h t) -> p b s h t", b=2, s=2, h=HG)
        v = v_f[:].rearrange("p (i n h c) -> p i n h c", i=PAIR, n=3, h=E * 12)
        XR, PR = 4, 3
        p_s = sb("p_s", [128, XR * HU * KWN[1]])
        sig = p_s[:, 0:4 * D].rearrange("p (t d) -> p t d", t=4)
        gated = p_s[:, 4 * D:8 * D].rearrange("p (t d) -> p t d", t=4)
        smin = sb("smin", [128, XR, HU])
        pt = sb("pt", [128, PR, 2, HU * KWN[1]], F16)
        o_raw = sb("o_raw", [128, 2, PAIR, HG, VW])
        o_rcp = sb("o_rcp", [128, 2, PAIR, HG, 1])
        o_e = sb("o_e", [128, 2, 4, 256])
        lg = sb("lg", [128, 4, E])
        top = sb("top", [128, 4, 1])
        onehot = sb("onehot", [128, 4, E])
        onehot_inv = sb("onehot_inv", [128, 4, E])
        oht = sb("oht", [E, TP], F16)
        GR = 3
        gel = sb("gel", [128, GR, TP])
        ht_f = sb("ht_f", [128, 2 * HM * TP], F16)
        ht = ht_f[:].rearrange("p (s m t) -> p s m t", s=2, m=HM)
        x_raw = ht_f[:].bitcast(F32).rearrange("p (k t) -> p k t", k=PKT)
        acc = sb("acc", [128, 4, D])

        bank = [ctx.enter_context(nc.psum_tensor(f"bank{n}", [128, 512], F32)) for n in range(8)]

        const_in = sem("const_in")
        stage_in = sem("stage_in")
        x_in = sem("x_in")
        y_out = sem("y_out")
        split_hi = sem("split_hi")
        split_lo = sem("split_lo")
        merge_mm = sem("merge_mm")
        names = """patch_mm z1_ready z2_ready z1t_mm z1t_hi z1t_lo z2t_mm z2t_hi z2t_lo var_ready rstd_ready
            proj_mm proj_hi proj_lo v_dup k_masked scores_mm min_ready shifted p_ready pt_mm pt_hi pt_lo pv_mm
            o_copied o_summed o_rcp_ready o_twice o_ready ot_mm ot_hi ot_lo gu_mm sig_ready dve_own h_moved
            lg_mm onehot_ready oht_mm oht_ready b2_mm acc_ready hid_mm gel_ready ht_hi ht_lo ffn_mm
            x_hi x_lo""".split()
        S = {n: sem(n) for n in names}
        nums = sorted(s.num for s in S.values())
        assert nums == list(range(nums[0], nums[0] + len(nums)))
        per_turn = range(nums[0], nums[-1] + 1)

        stage_a = v_f[:].bitcast(F32)
        stage_b = kmask_f[:].bitcast(F32)
        merge_a = qt_f[0:KB].bitcast(F32)
        merge_b = kt_f[0:KB].bitcast(F32)
        wo_raw = merge_a[:, 0:DB * E * 256].rearrange("p (k e i) -> p k e i", k=DB, e=E)
        wgu_raw = merge_b[:, 0:G * 2 * D].rearrange("p (g n) -> p g n", g=G)

        def flat(t, part, rows):
            a = t[0:rows, part]
            n = len(a.shape)
            return a if n == 2 else a.rearrange({3: "p a b -> p (a b)", 4: "p a b c -> p (a b c)"}[n])

        half1 = E * HID
        n_qkv, n_w2, n_wp, n_gate = 3 * 2 * E * D, E * HM * D, PKT * D, 2 * E
        splits = [
            (stage_a, 0, n_qkv, 128, wqkv, lambda s: flat(wqkv_s, s, 128), WSCALE, 0),
            (stage_b, 0, half1, 128, w1[:, 0:half1], lambda s: flat(w1_s, s, 128)[:, 0:half1], WSCALE, 0),
            (stage_b, half1, n_wp, 128, wp, lambda s: flat(wp_s, s, 128), WSCALE, 0),
            (stage_a, 0, n_w2, 128, w2, lambda s: flat(w2_s, s, 128), WSCALE, 1),
            (stage_b, 0, half1, 128, w1[:, half1:2 * half1],
             lambda s: flat(w1_s, s, 128)[:, half1:2 * half1], WSCALE, 3),
            (stage_b, half1, n_gate, 128, gate_w, lambda s: flat(gate_s, s, 128), WSCALE, 3),
            (stage_b, half1 + n_gate, D, E, b2, lambda s: b2_s[:, s, :], 1.0, 3),
        ]

        D_PASSES = ((0, 0, 0), (0, 0, 1), (1, 0, 0), (0, 1, 2), (1, 1, 2))

        def product(psum, passes):
            for n, (stat, mov) in enumerate(passes):
                mm = nc.tensor.matmul(psum, stat, mov, start=(n == 0), stop=(n == len(passes) - 1))
            return mm

        def patch_tile(tt):
            _, _, c0, rows = tile_of(tt)
            product(bank[tt][0:rows, 0:D], [(x_s[:, s, k, c0:c0 + rows], wp_s[:, m, k, :])
                                            for k in range(PKT) for s, m in ((0, 0), (0, 1), (1, 0))]
                    ).then_inc(S["patch_mm"], 1)

        def turn(pe, z, ready, b0, done):
            for tt in range(4):
                _, _, c0, rows = tile_of(tt)
                if ready:
                    pe.wait_ge(S[ready], tt + 1)
                for blk in range(2):
                    mm = nc.tensor.transpose(bank[b0 + blk][:, c0:c0 + rows],
                                             z[0:rows, tt, 128 * blk:128 * blk + 128], ident_s[0:rows, 0:rows])
            mm.then_inc(S[done], 1)

        def high_of(act, b0, target, done, his):
            act.wait_ge(S[done], 1)
            for blk in range(2):
                nc.scalar.copy(target[:, 2 * blk, :], bank[b0 + blk][:, 0:TP]).then_inc(S[his], 1)

        def low_of(dve, b0, target, his, los):
            dve.wait_ge(S[his], 1)
            nc.vector.tensor_tensor(target[:, 1, :], bank[b0][:, 0:TP], target[:, 0, :],
                                    ALU.subtract).then_inc(S[los], 1)
            dve.wait_ge(S[his], 2)
            nc.vector.tensor_tensor(target[64:128, 2, :], bank[b0 + 1][64:128, 0:TP], target[64:128, 2, :],
                                    ALU.subtract).then_inc(S[los], 1)

        class Chain:

            def __init__(self, dve):
                self.dve, self.n = dve, 0

            def __call__(self, ins):
                self.n += 1
                ins.then_inc(S["dve_own"], 1)
                self.dve.wait_ge(S["dve_own"], self.n)

        def moments(chain, src, tt):
            half, img, _, rows = tile_of(tt)
            chain(nc.vector.bn_stats(stats[0:rows, tt, :], src[0:rows, tt, :]))
            chain(nc.vector.bn_aggr(mv[0:rows, tt, :], stats[0:rows, tt, :]))
            if img == 1:
                nc.vector.tensor_scalar(veps[0:rows, 2 * half:2 * half + 2], mv[0:rows, tt - 1:tt + 1, 1],
                                        LN_EPS, None, ALU.add).then_inc(S["var_ready"], 1)

        def inverse_std(pool, times):
            for half in range(2):
                t0, rows = 2 * half, ROWS[half]
                pool.wait_ge(S["var_ready"], 2 * times + half + 1)
                nc.gpsimd.tensor_tensor(rstd[0:rows, t0:t0 + 2], veps[0:rows, t0:t0 + 2],
                                        power[0:rows, t0:t0 + 2], ALU.pow).then_inc(S["rstd_ready"], 1)

        def normalise(dve, times, src, z, ready, tt):
            half, _, _, rows = tile_of(tt)
            dve.wait_ge(S["rstd_ready"], 2 * times + half + 1)
            for z0, z_n, s0 in ((0, D, 0), (D, 64, 128)):
                ins = nc.vector.tensor_scalar(z[0:rows, tt, z0:z0 + z_n], src[0:rows, tt, s0:s0 + z_n],
                                              mv[0:rows, tt, 0:1], rstd[0:rows, tt:tt + 1], ALU.subtract,
                                              ALU.mult)
            ins.then_inc(S[ready], 1)

        def embed(dve, chain):
            for tt in range(4):
                half, _, _, rows = tile_of(tt)
                dve.wait_ge(S["patch_mm"], tt + 1)
                chain(nc.vector.scalar_tensor_tensor(out=h_next[0:rows, tt, :], in0=bank[tt][0:rows, 0:D],
                                                     scalar=INV, in1=tok_bias_s[0:rows, half, :],
                                                     op0=ALU.mult, op1=ALU.add))
                moments(chain, h_next, tt)
            for tt in range(4):
                normalise(dve, 0, h_next, z, "z1_ready", tt)

        def logits():
            for tt in range(4):
                _, _, c0, rows = tile_of(tt)
                mm = product(bank[6][0:rows, E * tt:E * tt + E],
                             [(zt2[:, zi, c0:c0 + rows], gate_s[:, s, blk, :]) for s, blk, zi in D_PASSES])
            mm.then_inc(S["lg_mm"], 1)

        def choose(dve, chain):
            dve.wait_ge(S["lg_mm"], 1)
            for half in range(2):
                rows, t0 = ROWS[half], 2 * half
                lgh, toph = lg[0:rows, t0:t0 + 2, :], top[0:rows, t0:t0 + 2, :]
                oh = onehot[0:rows, t0:t0 + 2, :]
                wide = [rows, 2, E]
                chain(nc.vector.scalar_tensor_tensor(
                    out=lgh, in0=bank[6][0:rows, E * t0:E * t0 + 2 * E].rearrange("p (t e) -> p t e", e=E),
                    scalar=INV, in1=gate_bc_s[0:rows, 0:1, :].broadcast_to(wide), op0=ALU.mult, op1=ALU.add))
                chain(nc.vector.tensor_tensor(lgh, lgh, gate_bc_s[0:rows, 1:2, :].broadcast_to(wide),
                                              ALU.subtract))
                chain(nc.vector.reduce_max(toph, lgh, AX_X))
                chain(nc.vector.tensor_tensor(oh, lgh, toph.broadcast_to(wide), ALU.is_ge))
                chain(nc.vector.tensor_tensor(oh, oh, rank_s[0:rows, :].unsqueeze(1).broadcast_to(wide),
                                              ALU.mult))
                chain(nc.vector.reduce_max(toph, oh, AX_X))
                chain(nc.vector.tensor_tensor(oh, oh, toph.broadcast_to(wide), ALU.is_ge))
                nc.vector.tensor_scalar(onehot_inv[0:rows, t0:t0 + 2, :], oh, INV, None,
                                        ALU.mult).then_inc(S["onehot_ready"], 1)

        def turn_onehot(pe):
            pe.wait_ge(S["onehot_ready"], 2)
            for tt in range(4):
                _, _, c0, rows = tile_of(tt)
                mm = nc.tensor.transpose(bank[7][0:E, c0:c0 + rows], onehot[0:rows, tt, :],
                                         ident_s[0:rows, 0:rows])
            mm.then_inc(S["oht_mm"], 1)

        def copy_onehot(dve):
            dve.wait_ge(S["oht_mm"], 1)
            nc.vector.tensor_copy(oht[:], bank[7][0:E, 0:TP]).then_inc(S["oht_ready"], 1)

        def bias2(pe):
            pe.wait_ge(S["oht_ready"], 1)
            for tt in range(4):
                half, img, c0, rows = tile_of(tt)
                mm = product(bank[6 + half][0:rows, D * img:D * img + D],
                             [(oht[:, c0:c0 + rows], b2_s[:, s, :]) for s in range(2)])
                if img == 1:
                    mm.then_inc(S["b2_mm"], 1)

        def add_bias2(dve):
            for half in range(2):
                rows, t0 = ROWS[half], 2 * half
                dve.wait_ge(S["b2_mm"], half + 1)
                nc.vector.tensor_tensor(acc[0:rows, t0:t0 + 2, :], acc[0:rows, t0:t0 + 2, :],
                                        bank[6 + half][0:rows, 0:2 * D].rearrange("p (t d) -> p t d", t=2),
                                        ALU.add).then_inc(S["acc_ready"], 1)

        def hidden_mm(pe, e):
            for m in range(HM):
                a = HM * e + m
                if a >= 2:
                    pe.wait_ge(S["gel_ready"], a - 1)
                product(bank[5 + a % 2][:, 0:TP], [(w1_s[:, s, blk, e, 128 * m:128 * m + 128], zt2[:, zi, :])
                                                   for s, blk, zi in D_PASSES]).then_inc(S["hid_mm"], 1)

        def hidden_act(act, e):
            for m in range(HM):
                a = HM * e + m
                act.wait_ge(S["hid_mm"], a + 1)
                if a >= GR:
                    act.wait_ge(S["ht_lo"], a - GR + 1)
                nc.scalar.activation(gel[:, a % GR, :], bank[5 + a % 2][:, 0:TP], ACT.Gelu,
                                     bias=b1_s[:, e, m:m + 1], scale=INV).then_inc(S["gel_ready"], 1)

        def hidden_split(dve, e, in_loop):
            for m in range(HM):
                a = HM * e + m
                dve.wait_ge(S["gel_ready"], a + 1)
                if m == 0 and e == 0 and in_loop:
                    dve.wait_ge(S["x_lo"], 1)
                if m == 0 and e >= 1:
                    dve.wait_ge(S["ffn_mm"], 4 * e)
                nc.vector.tensor_copy(ht[:, 0, m, :], gel[:, a % GR, :]).then_inc(S["ht_hi"], 1)
                dve.wait_ge(S["ht_hi"], a + 1)
                nc.vector.tensor_tensor(ht[:, 1, m, :], gel[:, a % GR, :], ht[:, 0, m, :],
                                        ALU.subtract).then_inc(S["ht_lo"], 1)

        def expert_mm(pe, b):
            e, tt = b // 4, b % 4
            _, _, c0, rows = tile_of(tt)
            pe.wait_ge(S["ht_lo"], HM * (e + 1))
            pe.wait_ge(S["acc_ready"], 2 + b)
            product(bank[7][0:rows, 0:D], [(ht[:, s, m, c0:c0 + rows], w2_s[:, w, e, m, :])
                                           for m in range(HM) for s, w in ((0, 0), (0, 1), (1, 0))]
                    ).then_inc(S["ffn_mm"], 1)

        def add_expert(dve, b):
            e, tt = b // 4, b % 4
            rows = tile_of(tt)[3]
            dve.wait_ge(S["ffn_mm"], b + 1)
            dve.wait_ge(S["acc_ready"], 2 + b)
            nc.vector.scalar_tensor_tensor(out=acc[0:rows, tt, :], in0=bank[7][0:rows, 0:D],
                                           scalar=onehot_inv[0:rows, tt, e:e + 1], in1=acc[0:rows, tt, :],
                                           op0=ALU.mult, op1=ALU.add).then_inc(S["acc_ready"], 1)

        def store(sp, pair):
            for tt in range(4):
                half, img, _, rows = tile_of(tt)
                sp.wait_ge(S["acc_ready"], 2 + 4 * (E - 1) + tt + 1)
                sp.dma_start(out[pair, img, 128 * half:128 * half + rows, :],
                             acc[0:rows, tt, :]).then_inc(y_out, 16)

        with nc.Block() as block:
            @block.sync
            def _(sp):
                sp.dma_start(x_raw, x_t[0]).then_inc(x_in, 16)
                consts = [(ident_s, ident), (mask_id_s, mask_id), (masks_s, masks), (head_mask_s, head_mask),
                          (tok_bias_s, tok_bias), (b1_s, b1)]
                sp.dma_start(gate_bc_s[:], gate_bc).then_inc(y_out, 16)
                sp.dma_start(wo_raw, wo).then_inc(const_in, 16)
                sp.dma_start(wgu_raw, wgu).then_inc(const_in, 16)
                for n, (stage, c0, cols, rows, src, _, _, free) in enumerate(splits):
                    if free:
                        sp.wait_ge(split_lo, free)
                    sp.dma_start(stage[0:rows, c0:c0 + cols], src).then_inc(stage_in, 16)
                    sp.wait_ge(stage_in, 16 * (n + 1))
                for dst, src in consts:
                    sp.dma_start(dst[:], src).then_inc(const_in, 16)
                sp.wait_ge(const_in, 16 * (2 + len(consts)))

            @block.scalar
            def _(act):
                for n, (stage, c0, cols, rows, _, target, scale, _) in enumerate(splits):
                    act.wait_ge(stage_in, 16 * (n + 1))
                    nc.scalar.activation(target(0), stage[0:rows, c0:c0 + cols], ACT.Copy,
                                         scale=scale).then_inc(split_hi, 1)
                for g in range(2 * E):
                    act.wait_ge(merge_mm, g + 1)
                    nc.scalar.activation(wgu_s[:, 0, g, :], bank[g][:, 0:2 * D], ACT.Copy,
                                         scale=WSCALE).then_inc(split_hi, 1)
                act.wait_ge(x_in, 16)
                nc.scalar.copy(x_s[:, 0], x_raw).then_inc(split_hi, 1)

            @block.vector
            def _(dve):
                for n, (stage, c0, cols, rows, _, target, scale, _) in enumerate(splits):
                    dve.wait_ge(split_hi, n + 1)
                    nc.vector.scalar_tensor_tensor(out=target(1), in0=stage[0:rows, c0:c0 + cols],
                                                   scalar=scale, in1=target(0), op0=ALU.mult,
                                                   op1=ALU.subtract).then_inc(split_lo, 1)
                for g in range(2 * E):
                    dve.wait_ge(split_hi, len(splits) + g + 1)
                    nc.vector.scalar_tensor_tensor(out=wgu_s[:, 1, g, :], in0=bank[g][:, 0:2 * D],
                                                   scalar=WSCALE, in1=wgu_s[:, 0, g, :], op0=ALU.mult,
                                                   op1=ALU.subtract).then_inc(split_lo, 1)
                dve.wait_ge(split_hi, len(splits) + 2 * E + 1)
                nc.vector.tensor_tensor(x_s[:, 1], x_raw, x_s[:, 0], ALU.subtract).then_inc(split_lo, 1)
                dve.wait_ge(split_lo, 4)
                nc.vector.memset(v[:, :, :, :, 2 * HD:VW], 1.0)
                nc.vector.memset(power[:], -0.5)
                for e in range(E):
                    nc.vector.memset(rank_s[:, e:e + 1], float(E - e))

            @block.tensor
            def _(pe):
                pe.wait_ge(const_in, 16 * 2)
                for g in range(2 * E):
                    e, i0 = g // 2, g % 2 * 128
                    for k in range(DB):
                        mm = nc.tensor.matmul(bank[g][:, 0:2 * D], wo_raw[:, k, e, i0:i0 + 128],
                                              wgu_raw[:, e * DB + k, :], start=(k == 0), stop=(k == DB - 1))
                    mm.then_inc(merge_mm, 1)

        with nc.Block() as block:
            @block.sync
            def _(sp):
                sp.dma_start(x_raw, x_t[1]).then_inc(x_in, 16)

            @block.tensor
            def _(pe):
                for tt in range(4):
                    patch_tile(tt)
                turn(pe, z, "z1_ready", 4, "z1t_mm")

            @block.scalar
            def _(act):
                high_of(act, 4, zt1, "z1t_mm", "z1t_hi")

            @block.gpsimd
            def _(pool):
                inverse_std(pool, 0)

            @block.vector
            def _(dve):
                embed(dve, Chain(dve))
                low_of(dve, 4, zt1, "z1t_hi", "z1t_lo")
                dve.wait_ge(S["z1t_mm"], 1)
                nc.vector.memset(z[:], 0.0)
                nc.vector.memset(acc[:], 0.0)

        nc.all_engine_barrier(sems_to_clear=per_turn)

        proj = [("k", 0), ("q", 0)] + [("v", n) for n in range(8)]
        for g in range(1, G):
            proj += [("k", g), ("q", g)]
        v_first, PB = 2, 6
        AT_LOGITS, AT_CHOOSE, AT_ONEHOT, AT_BIAS2, AT_ADD2 = 4, 6, 12, 16, 19

        def proj_psum(n):
            kind, j = proj[n]
            if kind == "v":
                return bank[n % PB][0:ROWS[j // 4], 0:2 * D]
            return bank[n % PB][0:KB, 0:TP]

        def proj_target(n, part):
            kind, j = proj[n]
            if kind == "v":
                half, img, _, rows = tile_of(j // 2)
                return v[0:rows, img, 2 * half, 24 * (j % 2):24 * (j % 2) + 24, part * HD:part * HD + HD]
            return (kt if kind == "k" else qt)[:, j, part, :]

        def proj_src(n):
            p = proj_psum(n)
            return p.rearrange("p (h d) -> p h d", d=HD) if proj[n][0] == "v" else p

        def proj_scale(n):
            return -INV * HD ** -0.5 if proj[n][0] == "q" else INV

        def o_bank(rows):
            return bank[4][0:rows, 0:PAIR * HG * VW].rearrange("p (i h c) -> p i h c", i=PAIR, h=HG)

        def p_slot(u):
            c0 = u % XR * HU * KWN[1]
            return p_s[0:ROWS[unit_of(u)[1]], c0:c0 + HU * KWN[unit_of(u)[1]]]

        def split_heads(ap):
            return ap.rearrange("p (h k) -> p h k", h=HU)

        def shift_on_dve(u):
            return u % 4 in DVE_SHIFTS

        LAG_T, LAG_PV = 2, 3
        LAG_OC, LAG_OR = 4, 5
        OT_STEP = 28
        HID_STEP = 1
        OUT_STEPS = (4, 7, 10, 13)
        PIPE = 16 * (E - 1) + OT_STEP + 1

        def window_at(s, lag):
            u = s - lag
            return u // 4 if 0 <= u < UNITS and u % 4 == 3 else None

        def hidden_at(s):
            return s // 16 if s < UNITS and s % 16 == HID_STEP else None

        def output_at(s):
            return 4 * (s // 16) + OUT_STEPS.index(s % 16) if 0 <= s < UNITS and s % 16 in OUT_STEPS else None

        def turned_at(s):
            return (s - OT_STEP) // 16 if s >= OT_STEP and (s - OT_STEP) % 16 == 0 else None

        with nc.Fori(0, STEPS) as i:
            with nc.Block(no_gpsimd_drain=True) as block:

                @block.sync
                def _(sp):
                    for img in range(PAIR):
                        sp.wait_ge(S["proj_lo"], v_first + 2 * img + 2)
                        sp.dma_start(v[0:69, img, 1], v[KW0[1]:128, img, 0]).then_inc(S["v_dup"], 16)
                    sp.wait_ge(S["ffn_mm"], 4 * E)
                    sp.dma_start(x_raw, x_t[(i + 2) % STEPS]).then_inc(x_in, 16)
                    store(sp, (i + (STEPS - 1)) % STEPS)

                @block.tensor
                def _(pe):
                    turn(pe, z, None, 6, "z2t_mm")
                    for n, (kind, j) in enumerate(proj):
                        if n == AT_LOGITS:
                            pe.wait_ge(S["z2t_lo"], 2)
                            logits()
                        if n == AT_ONEHOT:
                            turn_onehot(pe)
                        if n == AT_BIAS2:
                            bias2(pe)
                        if n >= PB:
                            pe.wait_ge(S["proj_lo"], n - PB + 1)
                        if kind == "v":
                            _, _, c0, rows = tile_of(j // 2)
                            w0 = 2 * D * (j % 2)
                            passes = [(zt1[:, zi, c0:c0 + rows], wqkv_s[:, s, 2, blk, w0:w0 + 2 * D])
                                      for s, blk, zi in D_PASSES]
                        else:
                            m = 0 if kind == "q" else 1
                            passes = [(wqkv_s[:, s, m, blk, KB * j:KB * j + KB], zt1[:, zi, :])
                                      for s, blk, zi in D_PASSES]
                        product(proj_psum(n), passes).then_inc(S["proj_mm"], 1)

                    def scores(u):
                        g, half, hh, img = unit_of(u)
                        q0, rows = TOK * img + QW[half], ROWS[half]
                        k0, kn = TOK * img + KW0[half], KWN[half]
                        if u % 8 == 0:
                            pe.wait_ge(S["k_masked"], 2 * (g + 1))
                        if u >= 2:
                            pe.wait_ge(S["p_ready"], u - 1)
                        ps = bank[u % 2][0:rows, 0:HU * kn]
                        m0 = half * HU * KWN[0]
                        product(ps, [(qt[:, g, s, q0:q0 + rows],
                                      kmask[0:KB, g % 2, m, HU * hh:HU * hh + HU, k0:k0 + kn])
                                     for s, m in ((0, 0), (0, 1), (1, 0))]
                                + [(mask_id_s[0:rows, 0:rows], masks_s[0:rows, m0:m0 + HU * kn])]
                                ).then_inc(S["scores_mm"], 1)

                    def turn_p(u):
                        _, half, _, _ = unit_of(u)
                        rows, kn, nk = ROWS[half], KWN[half], (128, 69)[half]
                        pe.wait_ge(S["p_ready"], u + 1)
                        if u >= 2:
                            pe.wait_ge(S["pt_lo"], u - 1)
                        for b in range(HU * kn // nk):
                            mm = nc.tensor.transpose(bank[2 + u % 2][0:nk, b * nk:b * nk + rows],
                                                     p_slot(u)[:, b * nk:b * nk + nk],
                                                     ident_s[0:rows, 0:rows])
                        mm.then_inc(S["pt_mm"], 1)

                    def times_v(u):
                        g, half, hh, img = unit_of(u)
                        w = u // 4
                        rows, nk = ROWS[half], (128, 69)[half]
                        pe.wait_ge(S["pt_lo"], u + 1)
                        if u == 4:
                            pe.wait_ge(S["v_dup"], 32)
                        if u % 4 == 0 and w >= 1:
                            pe.wait_ge(S["o_copied"], w)
                        for j in range(HU):
                            head = HG * g + HU * hh + j
                            passes = []
                            for b in range(1 + half):
                                c = ((1 + half) * j + b) * nk
                                passes += [(pt[0:nk, u % PR, s, c:c + rows], v[0:nk, img, half + b, head, :])
                                           for s in range(2)]
                            mm = product(o_bank(rows)[:, img, HU * hh + j, :], passes)
                        mm.then_inc(S["pv_mm"], 1)

                    def turn_o(e):
                        pe.wait_ge(S["o_ready"], 4 * e + 4)
                        for blk in range(2):
                            for tt in range(4):
                                _, _, c0, rows = tile_of(tt)
                                mm = nc.tensor.transpose(bank[5 + blk][:, c0:c0 + rows],
                                                         o_e[0:rows, e % 2, tt, 128 * blk:128 * blk + 128],
                                                         ident_s[0:rows, 0:rows])
                            mm.then_inc(S["ot_mm"], 1)

                    pe.wait_ge(S["proj_lo"], len(proj))
                    pe.wait_ge(S["acc_ready"], 2)
                    for s in range(PIPE):
                        if s < UNITS:
                            scores(s)
                        if 0 <= s - LAG_T < UNITS:
                            turn_p(s - LAG_T)
                        if 0 <= s - LAG_PV < UNITS:
                            times_v(s - LAG_PV)
                        e = hidden_at(s)
                        if e is not None:
                            if e >= 2:
                                pe.wait_ge(S["ot_lo"], 2 * (e - 1))
                            hidden_mm(pe, e)
                        b = output_at(s)
                        if b is not None:
                            expert_mm(pe, b)
                        e = turned_at(s)
                        if e is not None:
                            pe.wait_ge(S["gel_ready"], HM * min(e + 2, E))
                            if e >= 1:
                                pe.wait_ge(S["ot_lo"], 2 * e)
                            turn_o(e)

                    pe.wait_ge(S["pt_lo"], UNITS)
                    for tt in range(4):
                        patch_tile(tt)
                    pe.wait_ge(S["acc_ready"], 2 + 4 * E)
                    pe.wait_ge(S["ot_lo"], 2 * E)
                    for tt in range(4):
                        _, _, c0, rows = tile_of(tt)
                        product(bank[4 + tt][0:rows, 0:2 * D],
                                [(ot[:, e, zi, c0:c0 + rows], wgu_s[:, s, 2 * e + blk, :])
                                 for e in range(E) for s, blk, zi in D_PASSES]).then_inc(S["gu_mm"], 1)
                        if tt == 2:
                            turn(pe, z, "z1_ready", 0, "z1t_mm")

                @block.scalar
                def _(act):
                    nc.scalar.copy(h[:, 0:2], h_next[:, 0:2])
                    nc.scalar.copy(h[0:ROWS[1], 2:4], h_next[0:ROWS[1], 2:4]).then_inc(S["h_moved"], 1)
                    high_of(act, 6, zt2, "z2t_mm", "z2t_hi")
                    for n in range(len(proj)):
                        act.wait_ge(S["proj_mm"], n + 1)
                        nc.scalar.activation(proj_target(n, 0), proj_src(n), ACT.Copy,
                                             scale=proj_scale(n)).then_inc(S["proj_hi"], 1)
                        if n == PB:
                            act.wait_ge(x_in, 16 * i + 32)
                            nc.scalar.copy(x_s[:, 0], x_raw).then_inc(S["x_hi"], 1)
                    for s in range(PIPE):
                        w = window_at(s, LAG_OC)
                        if w is not None:
                            rows = ROWS[w % 2]
                            act.wait_ge(S["pv_mm"], 4 * w + 4)
                            if w >= 2:
                                act.wait_ge(S["o_ready"], w - 1)
                            nc.scalar.copy(o_raw[0:rows, w % 2], o_bank(rows)).then_inc(S["o_copied"], 1)
                        u = s - LAG_T
                        if 0 <= u < UNITS:
                            half = unit_of(u)[1]
                            nk, n = (128, 69)[half], HU * KWN[half]
                            act.wait_ge(S["pt_mm"], u + 1)
                            if u >= PR:
                                act.wait_ge(S["pv_mm"], u - PR + 1)
                            nc.scalar.copy(pt[0:nk, u % PR, 0, 0:n], bank[2 + u % 2][0:nk, 0:n]
                                           ).then_inc(S["pt_hi"], 1)
                        if s < UNITS:
                            half = unit_of(s)[1]
                            rows, kn = ROWS[half], KWN[half]
                            if shift_on_dve(s):
                                act.wait_ge(S["shifted"], 1 + sum(shift_on_dve(j) for j in range(s)))
                                ins = nc.scalar.activation(p_slot(s), p_slot(s), ACT.Exp, scale=-1.0)
                            else:
                                act.wait_ge(S["min_ready"], s + 1)
                                if s >= XR:
                                    act.wait_ge(S["pt_mm"], s - XR + 1)
                                for j in range(HU):
                                    ins = nc.scalar.activation(
                                        p_slot(s)[:, j * kn:j * kn + kn], bank[s % 2][0:rows, j * kn:j * kn + kn],
                                        ACT.Exp, scale=-1.0, bias=smin[0:rows, s % XR, j:j + 1])
                            ins.then_inc(S["p_ready"], 1)
                        e = hidden_at(s)
                        if e is not None:
                            hidden_act(act, e)
                        e = turned_at(s)
                        if e is not None:
                            for blk in range(2):
                                act.wait_ge(S["ot_mm"], 2 * e + blk + 1)
                                nc.scalar.copy(ot[:, e, 2 * blk, :], bank[5 + blk][:, 0:TP]
                                               ).then_inc(S["ot_hi"], 1)
                    for tt in range(4):
                        rows = tile_of(tt)[3]
                        act.wait_ge(S["gu_mm"], tt + 1)
                        nc.scalar.activation(sig[0:rows, tt, :], bank[4 + tt][0:rows, 0:D], ACT.Exp,
                                             scale=-INV).then_inc(S["sig_ready"], 1)
                        if tt == 2:
                            high_of(act, 0, zt1, "z1t_mm", "z1t_hi")

                @block.gpsimd
                def _(pool):
                    def mask_keys(g):
                        for s in range(2):
                            if s == 0 and g >= 2:
                                pool.wait_ge(S["scores_mm"], 8 * (g - 1))
                            nc.gpsimd.tensor_tensor(
                                kmask[0:KB, g % 2, s], kt[:, g, s, :].unsqueeze(1).broadcast_to([KB, HG, TP]),
                                head_mask_s[:].unsqueeze(2).broadcast_to([KB, HG, TP]),
                                ALU.mult).then_inc(S["k_masked"], 1)

                    def divide(w):
                        half, g = w % 2, w // 2
                        e, gp, rows = g // 2, g % 2, ROWS[half]
                        o = o_e[0:rows, e % 2, 2 * half:2 * half + 2]
                        mine = o[:, :, KB * gp:KB * gp + KB].rearrange("p t (h d) -> p t h d", d=HD)
                        pool.wait_ge(S["o_copied"], w + 1)
                        if e >= 2 and gp == 0:
                            pool.wait_ge(S["ot_mm"], 2 * (e - 1))
                        nc.gpsimd.tensor_tensor(mine, o_raw[0:rows, w % 2, :, :, 0:HD],
                                                o_raw[0:rows, w % 2, :, :, HD:2 * HD],
                                                ALU.add).then_inc(S["o_summed"], 1)
                        pool.wait_ge(S["o_summed"], w + 1)
                        pool.wait_ge(S["o_rcp_ready"], w + 1)
                        rcp = o_rcp[0:rows, w % 2]
                        if gp == 1:
                            twice = o[:, :, D:256].rearrange("p t (h d) -> p t h d", d=HD)
                            nc.gpsimd.tensor_tensor(twice, mine[:, :, 2:HG], rcp[:, :, 2:HG].broadcast_to(
                                [rows, PAIR, HG - 2, HD]), ALU.mult).then_inc(S["o_twice"], 1)
                            pool.wait_ge(S["o_twice"], 2 * e + half + 1)
                        nc.gpsimd.tensor_tensor(mine, mine, rcp.broadcast_to([rows, PAIR, HG, HD]),
                                                ALU.mult).then_inc(S["o_ready"], 1)

                    pool.wait_ge(S["proj_lo"], 1)
                    mask_keys(0)
                    pool.wait_ge(S["x_hi"], 1)
                    nc.gpsimd.tensor_tensor(x_s[:, 1], x_raw, x_s[:, 0], ALU.subtract).then_inc(S["x_lo"], 1)
                    pool.wait_ge(S["proj_lo"], len(proj))
                    for g in range(G):
                        if g + 1 < G:
                            mask_keys(g + 1)
                        if g >= 1:
                            divide(2 * g - 1)
                        divide(2 * g)
                    divide(2 * G - 1)
                    inverse_std(pool, 0)
                    inverse_std(pool, 1)

                @block.vector
                def _(dve):
                    chain = Chain(dve)
                    low_of(dve, 6, zt2, "z2t_hi", "z2t_lo")
                    for n in range(len(proj)):
                        dve.wait_ge(S["proj_hi"], n + 1)
                        nc.vector.scalar_tensor_tensor(out=proj_target(n, 1), in0=proj_src(n),
                                                       scalar=proj_scale(n), in1=proj_target(n, 0),
                                                       op0=ALU.mult, op1=ALU.subtract).then_inc(S["proj_lo"], 1)
                        if n == AT_CHOOSE:
                            choose(dve, chain)
                        if n == AT_ONEHOT + 1:
                            copy_onehot(dve)
                        if n == AT_ADD2:
                            add_bias2(dve)

                    shifts = 0
                    for s in range(PIPE):
                        if s < UNITS:
                            half = unit_of(s)[1]
                            rows, kn = ROWS[half], KWN[half]
                            ps = split_heads(bank[s % 2][0:rows, 0:HU * kn])
                            least = smin[0:rows, s % XR, :]
                            dve.wait_ge(S["scores_mm"], s + 1)
                            nc.vector.tensor_reduce(least, ps, AX_X, ALU.min).then_inc(S["min_ready"], 1)
                            if shift_on_dve(s):
                                dve.wait_ge(S["min_ready"], s + 1)
                                if s >= XR:
                                    dve.wait_ge(S["pt_mm"], s - XR + 1)
                                nc.vector.tensor_tensor(split_heads(p_slot(s)), ps,
                                                        least.unsqueeze(2).broadcast_to([rows, HU, kn]),
                                                        ALU.subtract).then_inc(S["shifted"], 1)
                        u = s - LAG_T
                        if 0 <= u < UNITS:
                            half = unit_of(u)[1]
                            nk, n = (128, 69)[half], HU * KWN[half]
                            dve.wait_ge(S["pt_hi"], u + 1)
                            nc.vector.tensor_tensor(pt[0:nk, u % PR, 1, 0:n], bank[2 + u % 2][0:nk, 0:n],
                                                    pt[0:nk, u % PR, 0, 0:n], ALU.subtract
                                                    ).then_inc(S["pt_lo"], 1)
                        w = window_at(s, LAG_OR)
                        if w is not None:
                            rows = ROWS[w % 2]
                            dve.wait_ge(S["o_copied"], w + 1)
                            if w >= 2:
                                dve.wait_ge(S["o_ready"], w - 1)
                            nc.vector.reciprocal(o_rcp[0:rows, w % 2], o_raw[0:rows, w % 2, :, :, 2 * HD:VW]
                                                 ).then_inc(S["o_rcp_ready"], 1)
                        e = hidden_at(s)
                        if e is not None:
                            hidden_split(dve, e, True)
                        b = output_at(s - 1)
                        if b is not None:
                            add_expert(dve, b)
                        e = turned_at(s)
                        if e is not None:
                            dve.wait_ge(S["ot_hi"], 2 * e + 1)
                            nc.vector.tensor_tensor(ot[:, e, 1, :], bank[5][:, 0:TP], ot[:, e, 0, :],
                                                    ALU.subtract).then_inc(S["ot_lo"], 1)
                            dve.wait_ge(S["ot_hi"], 2 * e + 2)
                            nc.vector.tensor_tensor(ot[64:128, e, 2, :], bank[6][64:128, 0:TP],
                                                    ot[64:128, e, 2, :], ALU.subtract).then_inc(S["ot_lo"], 1)

                    embed(dve, chain)
                    dve.wait_ge(S["h_moved"], 1)
                    dve.wait_ge(y_out, 64 * i + 80)
                    for tt in range(4):
                        rows = tile_of(tt)[3]
                        sg, gu = sig[0:rows, tt, :], gated[0:rows, tt, :]
                        dve.wait_ge(S["sig_ready"], tt + 1)
                        chain(nc.vector.tensor_scalar(sg, sg, 1.0, None, ALU.add))
                        chain(nc.vector.reciprocal(sg, sg))
                        chain(nc.vector.scalar_tensor_tensor(out=gu, in0=bank[4 + tt][0:rows, 0:D], scalar=INV,
                                                             in1=sg, op0=ALU.mult, op1=ALU.mult))
                        chain(nc.vector.scalar_tensor_tensor(out=gu, in0=bank[4 + tt][0:rows, D:2 * D],
                                                             scalar=INV, in1=gu, op0=ALU.mult, op1=ALU.mult))
                        chain(nc.vector.tensor_tensor(acc[0:rows, tt, :], h[0:rows, tt, :], gu, ALU.add))
                        moments(chain, acc, tt)
                        if tt == 2:
                            low_of(dve, 0, zt1, "z1t_hi", "z1t_lo")
                    dve.wait_ge(S["z1t_mm"], 1)
                    for tt in range(4):
                        normalise(dve, 1, acc, z, "z2_ready", tt)

            nc.all_engine_barrier(sems_to_clear=per_turn)

        with nc.Block() as block:
            @block.sync
            def _(sp):
                store(sp, STEPS - 1)
                sp.wait_ge(y_out, 64 * STEPS + 80)

            @block.tensor
            def _(pe):
                turn(pe, z, None, 6, "z2t_mm")
                pe.wait_ge(S["z2t_lo"], 2)
                logits()
                turn_onehot(pe)
                bias2(pe)
                for e in range(E):
                    if e == 0:
                        pe.wait_ge(S["acc_ready"], 2)
                    hidden_mm(pe, e)
                    for tt in range(4):
                        expert_mm(pe, 4 * e + tt)

            @block.scalar
            def _(act):
                high_of(act, 6, zt2, "z2t_mm", "z2t_hi")
                for e in range(E):
                    hidden_act(act, e)

            @block.vector
            def _(dve):
                low_of(dve, 6, zt2, "z2t_hi", "z2t_lo")
                choose(dve, Chain(dve))
                copy_onehot(dve)
                add_bias2(dve)
                for e in range(E):
                    hidden_split(dve, e, False)
                    for tt in range(4):
                        add_expert(dve, 4 * e + tt)


def layouts(x, cls_tok, L0_tok_W_proj, L0_tok_b_proj, L0_attn_wq, L0_attn_wk, L0_attn_wv, L0_attn_wo,
            L0_attn_w_gate, L0_attn_w_up, L0_ffn_gate_w, L0_ffn_gate_b, L0_ffn_gate_center, L0_ffn_w1,
            L0_ffn_b1, L0_ffn_w2, L0_ffn_b2):
    import numpy as np
    f = np.float32

    def rows(a, kb):
        return a.reshape(-1, kb, *a.shape[1:]).swapaxes(0, 1)

    def packed(a):
        return np.stack([a[0:128], np.concatenate([a[128:D], a[128:D]])], 1)

    p = x.reshape(IMGS, 3, 14, 16, 14, 16).transpose(1, 3, 5, 0, 2, 4).reshape(PATCH, STEPS, PAIR, TOK - 1)
    x_t = np.zeros((STEPS, 128, PKT, PAIR, TOK), f)
    x_t[..., 1:] = p.reshape(PKT, 128, STEPS, PAIR, TOK - 1).transpose(2, 1, 0, 3, 4)
    tok_bias = np.empty((128, 2, D), f)
    tok_bias[:] = L0_tok_b_proj
    tok_bias[0, 0] = cls_tok[0, 0]
    gate_bc = np.empty((128, 2, E), f)
    gate_bc[:, 0] = L0_ffn_gate_b
    gate_bc[:, 1] = L0_ffn_gate_center
    wqkv = np.stack([packed(w.transpose(2, 0, 1).reshape(D, E * D))
                     for w in (L0_attn_wq, L0_attn_wk, L0_attn_wv)], 1)
    wgu = np.concatenate([L0_attn_w_gate.T, L0_attn_w_up.T], 1)
    masks = []
    for half in range(2):
        q = QW[half] + np.arange(128)[:, None]
        k = KW0[half] + np.arange(KWN[half])[None, :]
        m = np.where((q - k >= 0) & (q - k < WIN), 0.0, MASKED)
        masks.append(np.tile(m, (1, HU)))
    c = np.ascontiguousarray
    return dict(
        x_t=x_t.reshape(STEPS, 128, PKT, TP),
        wp=c(rows(L0_tok_W_proj.T, 128).reshape(128, -1)),
        tok_bias=tok_bias,
        wqkv=c(wqkv.reshape(128, -1)),
        wo=c(rows(packed(L0_attn_wo.transpose(2, 1, 0)).transpose(2, 3, 1, 0).reshape(D, E, 256), KB)),
        wgu=c(rows(wgu, KB)),
        gate_w=c(packed(L0_ffn_gate_w).reshape(128, -1)),
        gate_bc=gate_bc,
        w1=c(packed(L0_ffn_w1.transpose(1, 0, 2)).reshape(128, -1)),
        b1=c(L0_ffn_b1.reshape(E, HM, 128).transpose(2, 0, 1)),
        w2=c(L0_ffn_w2.reshape(E, HM, 128, D).transpose(2, 0, 1, 3).reshape(128, -1)),
        b2=c(L0_ffn_b2),
        ident=np.eye(128, dtype=f),
        mask_id=(MASK_ID * np.eye(128)).astype(np.float16),
        masks=np.concatenate(masks, 1).astype(np.float16),
        head_mask=np.kron(np.eye(HG), np.ones((HD, 1))).astype(np.float16),
    )


def kernel(**inputs):
    import numpy as np
    from concourse import bacc
    from concourse.bass_utils import run_bass_kernel_spmd

    arrays = layouts(**{k: np.asarray(a) for k, a in inputs.items()})
    nc = bacc.Bacc("TRN2", target_bir_lowering=False, num_devices=1)
    args = {n: nc.dram_tensor(f"{n}_dram", a.shape, mybir.dt.from_np(a.dtype), kind="ExternalInput").ap()
            for n, a in arrays.items()}
    out = nc.dram_tensor("out_dram", (STEPS, PAIR, TOK, D), F32, kind="ExternalOutput").ap()
    vit_layer(nc, **args, out=out)
    r = run_bass_kernel_spmd(nc, [{f"{n}_dram": a for n, a in arrays.items()}], core_ids=[0])
    return r.results[0]["out_dram"].reshape(IMGS, TOK, D)
```

```python
from contextlib import ExitStack

import concourse.bass as bass
from concourse import mybir

F32 = mybir.dt.float32
F16 = mybir.dt.float16
ALU = mybir.AluOpType
ACT = mybir.ActivationFunctionType
AX_X = mybir.AxisListType.X

IMGS = 64
PAIR = 2
STEPS = IMGS // PAIR
TOK = 197
TP = PAIR * TOK
D = 192
KB = 96
DB = D // KB
PATCH = 768
PKT = PATCH // 128
E = 4
HD = 16
G = E * D // KB
HG = KB // HD
HU = HG // 2
HP = HG // 2
QKP = E * D // 128
KS, QS = 3, 2
VW = 2 * HD + 1
WIN = 64
HID = 768
HM = HID // 128
ROWS = (128, TOK - 128)
QW = (0, 128)
KW0 = (0, TOK - 2 * 69)
KWN = (128, 138)
UNITS = G * 8
WSCALE = 256.0
INV = 1.0 / WSCALE
MASKED = 61440.0
MASK_ID = 16384.0
LN_EPS = 1e-5


def tile_of(tt):
    half, img = tt // 2, tt % 2
    return half, img, TOK * img + 128 * half, ROWS[half]


def unit_of(u):
    return u // 8, u // 4 % 2, u // 2 % 2, u % 2


def place_of(g):
    return HP * (g // 4), g % 4


def vit_layer(nc, x_t, wp, tok_bias, wqkv, wo, wgu, gate_w, gate_bc, w1, b1, w2, b2, ident, mask_id,
              masks, out):
    with ExitStack() as ctx:
        def sb(name, shape, dt=F32):
            return ctx.enter_context(nc.sbuf_tensor(name, shape, dt))

        def sem(name):
            return ctx.enter_context(nc.semaphore(name))

        wp_s = sb("wp_s", [128, 2, PKT, D], F16)
        wqkv_s = sb("wqkv_s", [128, 2, 3, 2, E * D], F16)
        wgu_s = sb("wgu_s", [128, 2, 2 * E, 2 * D], F16)
        w1_s = sb("w1_s", [128, 2, 2, E, HID], F16)
        w2_s = sb("w2_s", [128, 2, E, HM, D], F16)
        gate_s = sb("gate_s", [128, 2, 2, E], F16)
        b2_s = sb("b2_s", [E, 2, D], F16)
        b1_s = sb("b1_s", [128, E, HM])
        tok_bias_s = sb("tok_bias_s", [128, 2, D])
        gate_bc_s = sb("gate_bc_s", [128, 2, E])
        rank_s = sb("rank_s", [128, E])
        ident_s = sb("ident_s", [128, 128])
        mask_id_s = sb("mask_id_s", [128, 128], F16)
        masks_s = sb("masks_s", [128, HU * sum(KWN)], F16)

        x_s = sb("x_s", [128, 2, PKT, TP], F16)
        h_next = sb("h_next", [128, 4, D])
        h = sb("h", [128, 4, D])
        z = sb("z", [128, 4, 256])
        zt1 = sb("zt1", [128, 3, TP], F16)
        zt2 = sb("zt2", [128, 3, TP], F16)
        stats = sb("stats", [128, 4, 6])
        mv = sb("mv", [128, 4, 2])
        veps = sb("veps", [128, 4])
        rstd = sb("rstd", [128, 4])
        power = sb("power", [128, 4])
        qt_f = sb("qt_f", [128, 2 * QKP * TP], F16)
        kt_f = sb("kt_f", [128, max(2 * QKP * TP, 2 * G * 2 * D)], F16)
        stacks_f = sb("stacks_f", [128, (KS * HG + QS * HP) * TP], F16)
        v_f = sb("v_f", [128, PAIR * 3 * E * 12 * VW], F16)
        qt = qt_f[:].rearrange("p (g s t) -> p g s t", s=2, g=QKP)
        kt = kt_f[:, 0:2 * QKP * TP].rearrange("p (g s t) -> p g s t", s=2, g=QKP)
        ot = qt_f[:].rearrange("p (e c t) -> p e c t", e=E, c=3)
        kst = stacks_f[:, 0:KS * HG * TP].rearrange("p (b h t) -> p b h t", b=KS, h=HG)
        qst = stacks_f[:, KS * HG * TP:].rearrange("p (b h t) -> p b h t", b=QS, h=HP)
        v = v_f[:].rearrange("p (i n h c) -> p i n h c", i=PAIR, n=3, h=E * 12)
        XR, PR = 3, 4
        p_s = sb("p_s", [128, XR * HU * KWN[1]])
        sig = p_s[:, 0:4 * D].rearrange("p (t d) -> p t d", t=4)
        smin = sb("smin", [128, XR, HU])
        pt_f = sb("pt_f", [128, PR * 2 * HU * KWN[1]], F16)
        pt = pt_f[:].rearrange("p (r s n) -> p r s n", r=PR, s=2)
        gated = pt_f[:, 0:8 * D].bitcast(F32).rearrange("p (t d) -> p t d", t=4)
        o_raw = sb("o_raw", [128, 2, PAIR, HG, VW])
        o_rcp = sb("o_rcp", [128, 2, PAIR, HG, 1])
        o_e = sb("o_e", [128, 2, 4, 256])
        lg = sb("lg", [128, 4, E])
        top = sb("top", [128, 4, 1])
        onehot = sb("onehot", [128, 4, E])
        onehot_inv = sb("onehot_inv", [128, 4, E])
        oht = sb("oht", [E, TP], F16)
        GR = 5
        gel = sb("gel", [128, GR, TP])
        ht_f = sb("ht_f", [128, 2 * HM * TP], F16)
        ht = ht_f[:].rearrange("p (s m t) -> p s m t", s=2, m=HM)
        x_raw = ht_f[:].bitcast(F32).rearrange("p (k t) -> p k t", k=PKT)
        acc = sb("acc", [128, 4, D])

        bank = [ctx.enter_context(nc.psum_tensor(f"bank{n}", [128, 512], F32)) for n in range(8)]

        const_in = sem("const_in")
        stage_in = sem("stage_in")
        x_in = sem("x_in")
        y_out = sem("y_out")
        split_hi = sem("split_hi")
        split_lo = sem("split_lo")
        merge_mm = sem("merge_mm")
        names = """patch_mm embedded z1_ready z2_ready z1t_mm z1t_hi z1t_lo z2t_mm z2t_hi z2t_lo var_ready rstd_ready
            proj_mm proj_hi proj_lo v_dup stacked0 stacked1 stacked2 scores_mm min_ready p_ready pt_mm pt_hi pt_lo pv_mm
            o_copied o_summed o_rcp_ready o_twice o_ready ot_mm ot_hi ot_lo gu_mm sig_ready dve_own h_moved
            lg_mm onehot_ready oht_mm oht_ready b2_mm acc_ready hid_mm gel_ready ht_hi ht_lo ht_lo_dve ffn_mm
            x_hi x_lo""".split()
        S = {n: sem(n) for n in names}
        nums = sorted(s.num for s in S.values())
        assert nums == list(range(nums[0], nums[0] + len(nums)))
        per_turn = range(nums[0], nums[-1] + 1)

        stage_a = v_f[:].bitcast(F32)
        stage_b = stacks_f[:].bitcast(F32)
        merge_a = qt_f[0:KB].bitcast(F32)
        merge_b = kt_f[0:KB].bitcast(F32)
        wo_raw = merge_a[:, 0:DB * E * 256].rearrange("p (k e i) -> p k e i", k=DB, e=E)
        wgu_raw = merge_b[:, 0:G * 2 * D].rearrange("p (g n) -> p g n", g=G)

        def flat(t, part, rows):
            a = t[0:rows, part]
            n = len(a.shape)
            return a if n == 2 else a.rearrange({3: "p a b -> p (a b)", 4: "p a b c -> p (a b c)"}[n])

        half1 = E * HID
        n_qkv, n_w2, n_wp, n_gate = 3 * 2 * E * D, E * HM * D, PKT * D, 2 * E
        splits = [
            (stage_a, 0, n_qkv, 128, wqkv, lambda s: flat(wqkv_s, s, 128), WSCALE, 0),
            (stage_b, 0, half1, 128, w1[:, 0:half1], lambda s: flat(w1_s, s, 128)[:, 0:half1], WSCALE, 0),
            (stage_b, half1, n_wp, 128, wp, lambda s: flat(wp_s, s, 128), WSCALE, 0),
            (stage_a, 0, n_w2, 128, w2, lambda s: flat(w2_s, s, 128), WSCALE, 1),
            (stage_b, 0, half1, 128, w1[:, half1:2 * half1],
             lambda s: flat(w1_s, s, 128)[:, half1:2 * half1], WSCALE, 3),
            (stage_b, half1, n_gate, 128, gate_w, lambda s: flat(gate_s, s, 128), WSCALE, 3),
            (stage_b, half1 + n_gate, D, E, b2, lambda s: b2_s[:, s, :], 1.0, 3),
        ]

        D_PASSES = ((0, 0, 0), (0, 0, 1), (1, 0, 0), (0, 1, 2), (1, 1, 2))

        def product(psum, passes):
            for n, (stat, mov) in enumerate(passes):
                mm = nc.tensor.matmul(psum, stat, mov, start=(n == 0), stop=(n == len(passes) - 1))
            return mm

        PATCH_BANK, PATCH_PARTS = 7, 6

        def patch_psum(tt):
            return bank[PATCH_BANK][0:tile_of(tt)[3], D * (tt % 2):D * (tt % 2) + D]

        def patch_part(pe, n):
            tt, part = divmod(n, PATCH_PARTS)
            _, _, c0, rows = tile_of(tt)
            if part == 0 and tt == 2:
                pe.wait_ge(S["embedded"], 1)
            passes = [(x_s[:, s, k, c0:c0 + rows], wp_s[:, m, k, :])
                      for k in range(PKT) for s, m in ((0, 0), (0, 1), (1, 0))]
            size = len(passes) // PATCH_PARTS
            for p in range(size * part, size * part + size):
                mm = nc.tensor.matmul(patch_psum(tt), *passes[p], start=(p == 0), stop=(p == len(passes) - 1))
            if part == PATCH_PARTS - 1:
                mm.then_inc(S["patch_mm"], 1)

        def turn(pe, z, ready, b0, done):
            for tt in range(4):
                _, _, c0, rows = tile_of(tt)
                if ready:
                    pe.wait_ge(S[ready], tt + 1)
                for blk in range(2):
                    mm = nc.tensor.transpose(bank[b0 + blk][:, c0:c0 + rows],
                                             z[0:rows, tt, 128 * blk:128 * blk + 128], ident_s[0:rows, 0:rows])
            mm.then_inc(S[done], 1)

        def high_of(act, b0, target, done, his):
            act.wait_ge(S[done], 1)
            for blk in range(2):
                nc.scalar.copy(target[:, 2 * blk, :], bank[b0 + blk][:, 0:TP]).then_inc(S[his], 1)

        def low_of(dve, b0, target, his, los):
            dve.wait_ge(S[his], 1)
            nc.vector.tensor_tensor(target[:, 1, :], bank[b0][:, 0:TP], target[:, 0, :],
                                    ALU.subtract).then_inc(S[los], 1)
            dve.wait_ge(S[his], 2)
            nc.vector.tensor_tensor(target[64:128, 2, :], bank[b0 + 1][64:128, 0:TP], target[64:128, 2, :],
                                    ALU.subtract).then_inc(S[los], 1)

        class Chain:

            def __init__(self, dve):
                self.dve, self.n = dve, 0

            def __call__(self, ins):
                self.n += 1
                ins.then_inc(S["dve_own"], 1)
                self.dve.wait_ge(S["dve_own"], self.n)

        def moments(chain, src, tt):
            half, img, _, rows = tile_of(tt)
            chain(nc.vector.bn_stats(stats[0:rows, tt, :], src[0:rows, tt, :]))
            chain(nc.vector.bn_aggr(mv[0:rows, tt, :], stats[0:rows, tt, :]))
            if img == 1:
                nc.vector.tensor_scalar(veps[0:rows, 2 * half:2 * half + 2], mv[0:rows, tt - 1:tt + 1, 1],
                                        LN_EPS, None, ALU.add).then_inc(S["var_ready"], 1)

        def inverse_std(pool, times):
            for half in range(2):
                t0, rows = 2 * half, ROWS[half]
                pool.wait_ge(S["var_ready"], 2 * times + half + 1)
                nc.gpsimd.tensor_tensor(rstd[0:rows, t0:t0 + 2], veps[0:rows, t0:t0 + 2],
                                        power[0:rows, t0:t0 + 2], ALU.pow).then_inc(S["rstd_ready"], 1)

        def normalise(dve, times, src, z, ready, tt):
            half, _, _, rows = tile_of(tt)
            dve.wait_ge(S["rstd_ready"], 2 * times + half + 1)
            for z0, z_n, s0 in ((0, D, 0), (D, 64, 128)):
                ins = nc.vector.tensor_scalar(z[0:rows, tt, z0:z0 + z_n], src[0:rows, tt, s0:s0 + z_n],
                                              mv[0:rows, tt, 0:1], rstd[0:rows, tt:tt + 1], ALU.subtract,
                                              ALU.mult)
            ins.then_inc(S[ready], 1)

        def add_token_bias(half):
            rows, t0 = ROWS[half], 2 * half
            return nc.vector.scalar_tensor_tensor(
                out=h_next[0:rows, t0:t0 + 2, :],
                in0=bank[PATCH_BANK][0:rows, 0:2 * D].rearrange("p (t d) -> p t d", t=2), scalar=INV,
                in1=tok_bias_s[0:rows, half:half + 1, :].broadcast_to([rows, 2, D]), op0=ALU.mult, op1=ALU.add)

        def logits():
            for tt in range(4):
                _, _, c0, rows = tile_of(tt)
                mm = product(bank[6][0:rows, E * tt:E * tt + E],
                             [(zt2[:, zi, c0:c0 + rows], gate_s[:, s, blk, :]) for s, blk, zi in D_PASSES])
            mm.then_inc(S["lg_mm"], 1)

        def choose(dve, chain):
            dve.wait_ge(S["lg_mm"], 1)
            for half in range(2):
                rows, t0 = ROWS[half], 2 * half
                lgh, toph = lg[0:rows, t0:t0 + 2, :], top[0:rows, t0:t0 + 2, :]
                oh = onehot[0:rows, t0:t0 + 2, :]
                wide = [rows, 2, E]
                chain(nc.vector.scalar_tensor_tensor(
                    out=lgh, in0=bank[6][0:rows, E * t0:E * t0 + 2 * E].rearrange("p (t e) -> p t e", e=E),
                    scalar=INV, in1=gate_bc_s[0:rows, 0:1, :].broadcast_to(wide), op0=ALU.mult, op1=ALU.add))
                chain(nc.vector.tensor_tensor(lgh, lgh, gate_bc_s[0:rows, 1:2, :].broadcast_to(wide),
                                              ALU.subtract))
                chain(nc.vector.reduce_max(toph, lgh, AX_X))
                chain(nc.vector.tensor_tensor(oh, lgh, toph.broadcast_to(wide), ALU.is_ge))
                chain(nc.vector.tensor_tensor(oh, oh, rank_s[0:rows, :].unsqueeze(1).broadcast_to(wide),
                                              ALU.mult))
                chain(nc.vector.reduce_max(toph, oh, AX_X))
                chain(nc.vector.tensor_tensor(oh, oh, toph.broadcast_to(wide), ALU.is_ge))
                nc.vector.tensor_scalar(onehot_inv[0:rows, t0:t0 + 2, :], oh, INV, None,
                                        ALU.mult).then_inc(S["onehot_ready"], 1)

        def turn_onehot(pe):
            pe.wait_ge(S["onehot_ready"], 2)
            for tt in range(4):
                _, _, c0, rows = tile_of(tt)
                mm = nc.tensor.transpose(bank[7][0:E, c0:c0 + rows], onehot[0:rows, tt, :],
                                         ident_s[0:rows, 0:rows])
            mm.then_inc(S["oht_mm"], 1)

        def copy_onehot(dve):
            dve.wait_ge(S["oht_mm"], 1)
            nc.vector.tensor_copy(oht[:], bank[7][0:E, 0:TP]).then_inc(S["oht_ready"], 1)

        def bias2(pe):
            pe.wait_ge(S["oht_ready"], 1)
            for tt in range(4):
                half, img, c0, rows = tile_of(tt)
                mm = product(bank[6 + half][0:rows, D * img:D * img + D],
                             [(oht[:, c0:c0 + rows], b2_s[:, s, :]) for s in range(2)])
                if img == 1:
                    mm.then_inc(S["b2_mm"], 1)

        def add_bias2(dve):
            for half in range(2):
                rows, t0 = ROWS[half], 2 * half
                dve.wait_ge(S["b2_mm"], half + 1)
                nc.vector.tensor_tensor(acc[0:rows, t0:t0 + 2, :], h[0:rows, t0:t0 + 2, :],
                                        bank[6 + half][0:rows, 0:2 * D].rearrange("p (t d) -> p t d", t=2),
                                        ALU.add).then_inc(S["acc_ready"], 1)

        HID_BANK, OUT_BANK, EARLY = 6, 4, 3

        def hidden_mm(pe, a):
            e, m = divmod(a, HM)
            if a >= 2:
                pe.wait_ge(S["gel_ready"], a - 1)
            product(bank[HID_BANK + a % 2][:, 0:TP],
                    [(w1_s[:, s, blk, e, 128 * m:128 * m + 128], zt2[:, zi, :]) for s, blk, zi in D_PASSES]
                    ).then_inc(S["hid_mm"], 1)

        def expert_mm(pe, b):
            e, tt = b // 4, b % 4
            _, _, c0, rows = tile_of(tt)
            wait_low(pe, HM * e + HM - 1)
            wait_low(pe, HM * e + HM - 2)
            pe.wait_ge(S["acc_ready"], 2 + max(b - 1, 0))
            product(bank[OUT_BANK + b % 2][0:rows, 0:D], [(ht[:, s, m, c0:c0 + rows], w2_s[:, w, e, m, :])
                                                          for m in range(HM) for s, w in ((0, 0), (0, 1), (1, 0))]
                    ).then_inc(S["ffn_mm"], 1)

        def experts_pe(pe, turn_tokens):
            for m in range(HM):
                hidden_mm(pe, m)
            for e in range(E):
                if e + 1 < E:
                    for m in range(EARLY):
                        hidden_mm(pe, HM * (e + 1) + m)
                if e == E - 1 and turn_tokens:
                    turn(pe, z, "z2_ready", 0, "z2t_mm")
                for tt in range(4):
                    expert_mm(pe, 4 * e + tt)
                if e + 1 < E:
                    for m in range(EARLY, HM):
                        hidden_mm(pe, HM * (e + 1) + m)

        def gelu(act, a):
            e, m = divmod(a, HM)
            act.wait_ge(S["hid_mm"], a + 1)
            if a >= GR:
                wait_low(act, a - GR)
            nc.scalar.activation(gel[:, a % GR, :], bank[HID_BANK + a % 2][:, 0:TP], ACT.Gelu,
                                 bias=b1_s[:, e, m:m + 1], scale=INV).then_inc(S["gel_ready"], 1)

        def hidden_high(eng, copy, a):
            e, m = divmod(a, HM)
            if m == 0 and e >= 1:
                eng.wait_ge(S["ffn_mm"], 4 * e)
            eng.wait_ge(S["gel_ready"], a + 1)
            copy(ht[:, 0, m, :], gel[:, a % GR, :]).then_inc(S["ht_hi"], 1)

        def experts_act(act):
            for a in range(HM * E):
                gelu(act, a)
                if a < HM:
                    hidden_high(act, nc.scalar.copy, a)

        def low_on_dve(a):
            return a >= HM and a % 2 == 1

        def wait_low(eng, a):
            done = S["ht_lo_dve" if low_on_dve(a) else "ht_lo"]
            eng.wait_ge(done, sum(low_on_dve(n) == low_on_dve(a) for n in range(a + 1)))

        def hidden_low(eng, tensor_tensor, a):
            eng.wait_ge(S["ht_hi"], a + 1)
            tensor_tensor(ht[:, 1, a % HM, :], gel[:, a % GR, :], ht[:, 0, a % HM, :], ALU.subtract
                          ).then_inc(S["ht_lo_dve" if low_on_dve(a) else "ht_lo"], 1)

        def experts_pool(pool, e):
            for a in range(HM * e, HM * e + HM):
                if not low_on_dve(a):
                    hidden_low(pool, nc.gpsimd.tensor_tensor, a)

        def experts_dve(dve, e):
            for tt in range(4):
                add_expert(dve, 4 * e + tt)
            if e + 1 < E:
                for a in range(HM * (e + 1), HM * (e + 2)):
                    hidden_high(dve, nc.vector.tensor_copy, a)
                    if low_on_dve(a):
                        hidden_low(dve, nc.vector.tensor_tensor, a)

        def add_expert(dve, b):
            e, tt = b // 4, b % 4
            rows = tile_of(tt)[3]
            dve.wait_ge(S["ffn_mm"], b + 1)
            dve.wait_ge(S["acc_ready"], 2 + b)
            nc.vector.scalar_tensor_tensor(out=acc[0:rows, tt, :], in0=bank[OUT_BANK + b % 2][0:rows, 0:D],
                                           scalar=onehot_inv[0:rows, tt, e:e + 1], in1=acc[0:rows, tt, :],
                                           op0=ALU.mult, op1=ALU.add).then_inc(S["acc_ready"], 1)

        def store(sp, pair):
            for tt in range(4):
                half, img, _, rows = tile_of(tt)
                sp.wait_ge(S["acc_ready"], 2 + 4 * (E - 1) + tt + 1)
                sp.dma_start(out[pair, img, 128 * half:128 * half + rows, :],
                             acc[0:rows, tt, :]).then_inc(y_out, 16)

        with nc.Block() as block:
            @block.sync
            def _(sp):
                sp.dma_start(x_raw, x_t[0]).then_inc(x_in, 16)
                consts = [(ident_s, ident), (mask_id_s, mask_id), (masks_s, masks),
                          (tok_bias_s, tok_bias), (b1_s, b1)]
                sp.dma_start(gate_bc_s[:], gate_bc).then_inc(y_out, 16)
                sp.dma_start(wo_raw, wo).then_inc(const_in, 16)
                sp.dma_start(wgu_raw, wgu).then_inc(const_in, 16)
                for n, (stage, c0, cols, rows, src, _, _, free) in enumerate(splits):
                    if free:
                        sp.wait_ge(split_lo, free)
                    sp.dma_start(stage[0:rows, c0:c0 + cols], src).then_inc(stage_in, 16)
                    sp.wait_ge(stage_in, 16 * (n + 1))
                sp.wait_ge(const_in, 32)
                for dst, src in consts:
                    sp.dma_start(dst[:], src).then_inc(const_in, 16)
                sp.wait_ge(const_in, 16 * (2 + len(consts)))
                sp.wait_ge(y_out, 16)

            @block.scalar
            def _(act):
                for n, (stage, c0, cols, rows, _, target, scale, _) in enumerate(splits):
                    act.wait_ge(stage_in, 16 * (n + 1))
                    nc.scalar.activation(target(0), stage[0:rows, c0:c0 + cols], ACT.Copy,
                                         scale=scale).then_inc(split_hi, 1)
                for g in range(2 * E):
                    act.wait_ge(merge_mm, g + 1)
                    nc.scalar.activation(wgu_s[:, 0, g, :], bank[g][:, 0:2 * D], ACT.Copy,
                                         scale=WSCALE).then_inc(split_hi, 1)
                act.wait_ge(x_in, 16)
                nc.scalar.copy(x_s[:, 0], x_raw).then_inc(split_hi, 1)

            @block.vector
            def _(dve):
                for n, (stage, c0, cols, rows, _, target, scale, _) in enumerate(splits):
                    dve.wait_ge(split_hi, n + 1)
                    nc.vector.scalar_tensor_tensor(out=target(1), in0=stage[0:rows, c0:c0 + cols],
                                                   scalar=scale, in1=target(0), op0=ALU.mult,
                                                   op1=ALU.subtract).then_inc(split_lo, 1)
                for g in range(2 * E):
                    dve.wait_ge(split_hi, len(splits) + g + 1)
                    nc.vector.scalar_tensor_tensor(out=wgu_s[:, 1, g, :], in0=bank[g][:, 0:2 * D],
                                                   scalar=WSCALE, in1=wgu_s[:, 0, g, :], op0=ALU.mult,
                                                   op1=ALU.subtract).then_inc(split_lo, 1)
                dve.wait_ge(split_hi, len(splits) + 2 * E + 1)
                nc.vector.tensor_tensor(x_s[:, 1], x_raw, x_s[:, 0], ALU.subtract).then_inc(split_lo, 1)
                dve.wait_ge(split_lo, 4)
                nc.vector.memset(v[:, :, :, :, 2 * HD:VW], 1.0)
                nc.vector.memset(power[:], -0.5)
                for e in range(E):
                    nc.vector.memset(rank_s[:, e:e + 1], float(E - e))

            @block.tensor
            def _(pe):
                pe.wait_ge(const_in, 16 * 2)
                for g in range(2 * E):
                    e, i0 = g // 2, g % 2 * 128
                    for k in range(DB):
                        mm = nc.tensor.matmul(bank[g][:, 0:2 * D], wo_raw[:, k, e, i0:i0 + 128],
                                              wgu_raw[:, e * DB + k, :], start=(k == 0), stop=(k == DB - 1))
                    mm.then_inc(merge_mm, 1)

        with nc.Block() as block:
            @block.sync
            def _(sp):
                sp.dma_start(x_raw, x_t[1]).then_inc(x_in, 16)

            @block.tensor
            def _(pe):
                for n in range(4 * PATCH_PARTS):
                    patch_part(pe, n)
                turn(pe, z, "z1_ready", 4, "z1t_mm")

            @block.scalar
            def _(act):
                high_of(act, 4, zt1, "z1t_mm", "z1t_hi")

            @block.gpsimd
            def _(pool):
                inverse_std(pool, 0)

            @block.vector
            def _(dve):
                nc.vector.memset(stacks_f[:], 0.0)
                chain = Chain(dve)
                for half in range(2):
                    dve.wait_ge(S["patch_mm"], 2 * half + 2)
                    add_token_bias(half).then_inc(S["embedded"], 1)
                    dve.wait_ge(S["embedded"], half + 1)
                    for img in range(PAIR):
                        moments(chain, h_next, 2 * half + img)
                for tt in range(4):
                    normalise(dve, 0, h_next, z, "z1_ready", tt)
                low_of(dve, 4, zt1, "z1t_hi", "z1t_lo")
                nc.vector.memset(zt2[:], 0.0)
                nc.vector.memset(h[:], 0.0)

        nc.all_engine_barrier(sems_to_clear=per_turn)

        qk = [(kind, j) for j in range(QKP) for kind in ("k", "q")]
        proj = qk[:6] + [("v", n) for n in range(8)] + qk[6:]
        v_first, PB = 6, 6
        AT_LOGITS, AT_CHOOSE, AT_ONEHOT, AT_BIAS2, AT_ADD2 = 2, 3, 11, 16, 18

        def last_use(b):
            return max(n for n in range(len(proj)) if n % PB == b) + 1

        def proj_psum(n):
            kind, j = proj[n]
            if kind == "v":
                return bank[n % PB][0:ROWS[j // 4], 0:2 * D]
            return bank[n % PB][:, 0:TP]

        def proj_target(n, part):
            kind, j = proj[n]
            if kind == "v":
                half, img, _, rows = tile_of(j // 2)
                return v[0:rows, img, 2 * half, 24 * (j % 2):24 * (j % 2) + 24, part * HD:part * HD + HD]
            return (kt if kind == "k" else qt)[:, j, part, :]

        def proj_src(n):
            p = proj_psum(n)
            return p.rearrange("p (h d) -> p h d", d=HD) if proj[n][0] == "v" else p

        def proj_scale(n):
            return -INV * HD ** -0.5 if proj[n][0] == "q" else INV

        def projected(g):
            return 2 * HP if place_of(g)[0] == 0 else len(proj)

        def stacks_done(g):
            return 16 * 9 * (g // 3 + 1)

        def last_group_of_queries(e):
            last = (3 * (e + 1) - 1) // 2
            return max(g for g in range(G) if place_of(g)[0] <= last)

        SR, TR = 3, 3
        T_BANK, O_BANK, OT_BANK = SR, SR + TR, 7
        GU_BANKS = [u % SR for u in range(UNITS - SR, UNITS)] + [T_BANK] * (SR == 3)

        def o_bank(rows):
            return bank[O_BANK][0:rows, 0:PAIR * HG * VW].rearrange("p (i h c) -> p i h c", i=PAIR, h=HG)

        def p_slot(u):
            c0 = u % XR * HU * KWN[1]
            return p_s[0:ROWS[unit_of(u)[1]], c0:c0 + HU * KWN[unit_of(u)[1]]]

        def split_heads(ap):
            return ap.rearrange("p (h k) -> p h k", h=HU)

        LAG_T, LAG_HI, LAG_LO, LAG_PV = 2, 3, 4, 5
        LAG_OC, LAG_OR = 6, 7
        OT_STEP, OT_GAP, OT_HI, OT_LO = 25, 3, 1, 2
        PATCH_STEP, PATCH_GAP, PATCH_LAG = 0, 1, 1
        GU_STEPS = {64: 0, 69: 1, 70: 2, 74: 3}
        LN_STEPS = (70, 74)
        PIPE = 16 * (E - 1) + OT_STEP + OT_GAP + OT_LO + 1

        def window_at(s, lag):
            u = s - lag
            return u // 4 if 0 <= u < UNITS and u % 4 == 3 else None

        def patch_at(s):
            n, half = s - PATCH_STEP, 2 * PATCH_PARTS
            if 0 <= n < half:
                return n
            return n - PATCH_GAP if half <= n - PATCH_GAP < 2 * half else None

        def turned_at(s):
            e, left = divmod(s - OT_STEP, 16)
            return (e, left // OT_GAP) if 0 <= e < E and left in (0, OT_GAP) else None

        with nc.Fori(0, STEPS) as i:
            with nc.Block(no_gpsimd_drain=True) as block:

                @block.sync
                def _(sp):
                    def stack_queries(g):
                        sp.wait_ge(S["proj_lo"], projected(g))
                        if g >= QS:
                            sp.wait_ge(S["scores_mm"], 8 * (g - QS + 1))
                        j0, p = place_of(g)
                        for b in range(3):
                            sp.dma_start(qst[32 * b:32 * b + 32, g % QS],
                                         qt[32 * p:32 * p + 32, j0:j0 + HP, (0, 0, 1)[b]]
                                         ).then_inc(S[f"stacked{g % 3}"], 16)

                    def stack_keys(g):
                        sp.wait_ge(S["proj_lo"], projected(g))
                        if g >= KS:
                            sp.wait_ge(S["scores_mm"], 8 * (g - KS + 1))
                        j0, p = place_of(g)
                        for b in range(3):
                            for a in range(2):
                                r0, k0 = 32 * b + HD * a, 32 * p + HD * a
                                sp.dma_start(kst[r0:r0 + HD, g % KS, a:HG:2],
                                             kt[k0:k0 + HD, j0:j0 + HP, (0, 1, 0)[b]]
                                             ).then_inc(S[f"stacked{g % 3}"], 16)

                    stack_queries(0)
                    stack_keys(0)
                    for img in range(PAIR):
                        sp.wait_ge(S["proj_lo"], v_first + 2 * img + 2)
                        sp.dma_start(v[0:69, img, 1], v[KW0[1]:128, img, 0]).then_inc(S["v_dup"], 16)
                    stack_keys(1)
                    for g in range(1, G):
                        stack_queries(g)
                        if g + 1 < G:
                            stack_keys(g + 1)
                    store(sp, (i + (STEPS - 1)) % STEPS)

                @block.tensor
                def _(pe):
                    for n, (kind, j) in enumerate(proj):
                        if n == AT_LOGITS:
                            logits()
                        if n == AT_ONEHOT:
                            turn_onehot(pe)
                        if n == AT_BIAS2:
                            bias2(pe)
                        if n >= PB:
                            pe.wait_ge(S["proj_lo"], n - PB + 1)
                        if kind == "v":
                            _, _, c0, rows = tile_of(j // 2)
                            w0 = 2 * D * (j % 2)
                            passes = [(zt1[:, zi, c0:c0 + rows], wqkv_s[:, s, 2, blk, w0:w0 + 2 * D])
                                      for s, blk, zi in D_PASSES]
                        else:
                            m = 0 if kind == "q" else 1
                            passes = [(wqkv_s[:, s, m, blk, 128 * j:128 * j + 128], zt1[:, zi, :])
                                      for s, blk, zi in D_PASSES]
                        product(proj_psum(n), passes).then_inc(S["proj_mm"], 1)

                    def scores(u):
                        g, half, hh, img = unit_of(u)
                        q0, rows = TOK * img + QW[half], ROWS[half]
                        k0, kn = TOK * img + KW0[half], KWN[half]
                        if u % 8 == 0:
                            pe.wait_ge(S[f"stacked{g % 3}"], stacks_done(g))
                        if u >= SR:
                            pe.wait_ge(S["p_ready"], u - SR + 1)
                        else:
                            pe.wait_ge(S["proj_lo"], last_use(u))
                        ps = bank[u % SR][0:rows, 0:HU * kn]
                        m0 = half * HU * KWN[0]
                        nc.tensor.matmul(ps, mask_id_s[:, 0:rows], masks_s[:, m0:m0 + HU * kn],
                                         start=True, stop=False)
                        for two, j0, j1 in ((0, 0, 2), (1, 2, 3)) if hh == 0 else ((1, 0, 1), (2, 1, 3)):
                            h0 = HU * hh
                            mm = nc.tensor.matmul(ps[:, j0 * kn:j1 * kn], qst[:, g % QS, two, q0:q0 + rows],
                                                  kst[:, g % KS, h0 + j0:h0 + j1, k0:k0 + kn],
                                                  start=False, stop=(j1 == HU))
                        mm.then_inc(S["scores_mm"], 1)

                    def turn_p(u):
                        _, half, _, _ = unit_of(u)
                        rows, kn, nk = ROWS[half], KWN[half], (128, 69)[half]
                        pe.wait_ge(S["p_ready"], u + 1)
                        if u >= TR:
                            pe.wait_ge(S["pt_lo"], u - TR + 1)
                        else:
                            pe.wait_ge(S["proj_lo"], last_use(T_BANK + u))
                        for b in range(HU * kn // nk):
                            mm = nc.tensor.transpose(bank[T_BANK + u % TR][0:nk, b * nk:b * nk + rows],
                                                     p_slot(u)[:, b * nk:b * nk + nk],
                                                     ident_s[0:rows, 0:rows])
                        mm.then_inc(S["pt_mm"], 1)

                    def times_v(u):
                        g, half, hh, img = unit_of(u)
                        w = u // 4
                        rows, nk = ROWS[half], (128, 69)[half]
                        pe.wait_ge(S["pt_lo"], u + 1)
                        if u == 0:
                            pe.wait_ge(S["acc_ready"], 2)
                        if u == 4:
                            pe.wait_ge(S["v_dup"], 32)
                        if u % 4 == 0 and w >= 1:
                            pe.wait_ge(S["o_copied"], w)
                        for j in range(HU):
                            head = HG * g + HU * hh + j
                            passes = []
                            for b in range(1 + half):
                                c = ((1 + half) * j + b) * nk
                                passes += [(pt[0:nk, u % PR, s, c:c + rows], v[0:nk, img, half + b, head, :])
                                           for s in range(2)]
                            mm = product(o_bank(rows)[:, img, HU * hh + j, :], passes)
                        mm.then_inc(S["pv_mm"], 1)

                    def turn_o(e, blk):
                        pe.wait_ge(S["o_ready"], 4 * e + 4)
                        if 2 * e + blk > 0:
                            pe.wait_ge(S["ot_lo"], 2 * e + blk)
                        if e == 0:
                            pe.wait_ge(S["embedded"], 2)
                        for tt in range(4):
                            _, _, c0, rows = tile_of(tt)
                            mm = nc.tensor.transpose(bank[OT_BANK][:, c0:c0 + rows],
                                                     o_e[0:rows, e % 2, tt, 128 * blk:128 * blk + 128],
                                                     ident_s[0:rows, 0:rows])
                        mm.then_inc(S["ot_mm"], 1)

                    def gate_up(tt, experts):
                        _, _, c0, rows = tile_of(tt)
                        passes = [(ot[:, e, zi, c0:c0 + rows], wgu_s[:, s, 2 * e + blk, :])
                                  for e in range(E) for s, blk, zi in D_PASSES]
                        for n in range(len(D_PASSES) * experts[0], len(D_PASSES) * (experts[-1] + 1)):
                            mm = nc.tensor.matmul(bank[GU_BANKS[tt]][0:rows, 0:2 * D], *passes[n],
                                                  start=(n == 0), stop=(n == len(passes) - 1))
                        return mm

                    for s in range(PIPE):
                        if s < UNITS:
                            scores(s)
                        n = patch_at(s)
                        if n is not None:
                            if n == 0:
                                pe.wait_ge(S["x_lo"], 1)
                                pe.wait_ge(S["acc_ready"], 2)
                            patch_part(pe, n)
                        if 0 <= s - LAG_T < UNITS:
                            turn_p(s - LAG_T)
                        if 0 <= s - LAG_PV < UNITS:
                            times_v(s - LAG_PV)
                        if turned_at(s):
                            turn_o(*turned_at(s))
                        tt = GU_STEPS.get(s)
                        if tt is not None:
                            if tt == 0:
                                pe.wait_ge(S["ot_lo"], 2 * (E - 1))
                            if tt < SR:
                                pe.wait_ge(S["p_ready"], UNITS - SR + tt + 1)
                            else:
                                pe.wait_ge(S["pt_lo"], UNITS)
                            gate_up(tt, range(0, E - 1))

                    turn(pe, z, "z1_ready", OUT_BANK, "z1t_mm")
                    pe.wait_ge(S["ot_lo"], 2 * E)
                    for tt in range(4):
                        gate_up(tt, range(E - 1, E)).then_inc(S["gu_mm"], 1)
                    pe.wait_ge(S["z1t_lo"], 2)
                    experts_pe(pe, True)

                @block.scalar
                def _(act):
                    for n in range(len(proj)):
                        act.wait_ge(S["proj_mm"], n + 1)
                        nc.scalar.activation(proj_target(n, 0), proj_src(n), ACT.Copy,
                                             scale=proj_scale(n)).then_inc(S["proj_hi"], 1)
                        if n == PB:
                            act.wait_ge(x_in, 16 * i + 32)
                            nc.scalar.copy(x_s[:, 0], x_raw).then_inc(S["x_hi"], 1)
                    for s in range(PIPE):
                        u = s - LAG_HI
                        if 0 <= u < UNITS:
                            half = unit_of(u)[1]
                            nk, n = (128, 69)[half], HU * KWN[half]
                            act.wait_ge(S["pt_mm"], u + 1)
                            if u >= PR:
                                act.wait_ge(S["pv_mm"], u - PR + 1)
                            nc.scalar.copy(pt[0:nk, u % PR, 0, 0:n], bank[T_BANK + u % TR][0:nk, 0:n]
                                           ).then_inc(S["pt_hi"], 1)
                        if s < UNITS:
                            half = unit_of(s)[1]
                            rows, kn = ROWS[half], KWN[half]
                            act.wait_ge(S["min_ready"], s + 1)
                            if s >= XR:
                                act.wait_ge(S["pt_mm"], s - XR + 1)
                            for j in range(HU):
                                ins = nc.scalar.activation(
                                    p_slot(s)[:, j * kn:j * kn + kn], bank[s % SR][0:rows, j * kn:j * kn + kn],
                                    ACT.Exp, scale=-1.0, bias=smin[0:rows, s % XR, j:j + 1])
                            ins.then_inc(S["p_ready"], 1)
                        if turned_at(s - OT_HI):
                            e, blk = turned_at(s - OT_HI)
                            for g in range(last_group_of_queries(e) - 2, last_group_of_queries(e) + 1):
                                act.wait_ge(S[f"stacked{g % 3}"], stacks_done(g))
                            act.wait_ge(S["ot_mm"], 2 * e + blk + 1)
                            nc.scalar.copy(ot[:, e, 2 * blk, :], bank[OT_BANK][:, 0:TP]
                                           ).then_inc(S["ot_hi"], 1)
                    high_of(act, OUT_BANK, zt1, "z1t_mm", "z1t_hi")
                    for tt in range(4):
                        rows = tile_of(tt)[3]
                        act.wait_ge(S["gu_mm"], tt + 1)
                        nc.scalar.activation(sig[0:rows, tt, :], bank[GU_BANKS[tt]][0:rows, 0:D], ACT.Exp,
                                             scale=-INV).then_inc(S["sig_ready"], 1)
                    experts_act(act)
                    high_of(act, 0, zt2, "z2t_mm", "z2t_hi")
                    act.wait_ge(S["ffn_mm"], 4 * E)
                    act.dma_start(x_raw, x_t[(i + 2) % STEPS]).then_inc(x_in, 16)

                @block.gpsimd
                def _(pool):
                    def divide(w):
                        half, g = w % 2, w // 2
                        e, gp, rows = g // 2, g % 2, ROWS[half]
                        o = o_e[0:rows, e % 2, 2 * half:2 * half + 2]
                        mine = o[:, :, KB * gp:KB * gp + KB].rearrange("p t (h d) -> p t h d", d=HD)
                        pool.wait_ge(S["o_copied"], w + 1)
                        if e >= 2 and gp == 0:
                            pool.wait_ge(S["ot_mm"], 2 * (e - 1))
                        nc.gpsimd.tensor_tensor(mine, o_raw[0:rows, w % 2, :, :, 0:HD],
                                                o_raw[0:rows, w % 2, :, :, HD:2 * HD],
                                                ALU.add).then_inc(S["o_summed"], 1)
                        pool.wait_ge(S["o_summed"], w + 1)
                        pool.wait_ge(S["o_rcp_ready"], w + 1)
                        rcp = o_rcp[0:rows, w % 2]
                        if gp == 1:
                            twice = o[:, :, D:256].rearrange("p t (h d) -> p t h d", d=HD)
                            nc.gpsimd.tensor_tensor(twice, mine[:, :, 2:HG], rcp[:, :, 2:HG].broadcast_to(
                                [rows, PAIR, HG - 2, HD]), ALU.mult).then_inc(S["o_twice"], 1)
                            pool.wait_ge(S["o_twice"], 2 * e + half + 1)
                        nc.gpsimd.tensor_tensor(mine, mine, rcp.broadcast_to([rows, PAIR, HG, HD]),
                                                ALU.mult).then_inc(S["o_ready"], 1)

                    pool.wait_ge(S["x_hi"], 1)
                    nc.gpsimd.tensor_tensor(x_s[:, 1], x_raw, x_s[:, 0], ALU.subtract).then_inc(S["x_lo"], 1)
                    pool.wait_ge(S["acc_ready"], 2)
                    nc.gpsimd.tensor_copy(h[:, 0:2], h_next[:, 0:2])
                    nc.gpsimd.tensor_copy(h[0:ROWS[1], 2:4], h_next[0:ROWS[1], 2:4]).then_inc(S["h_moved"], 1)
                    for w in range(2 * G):
                        divide(w)
                    inverse_std(pool, 0)
                    experts_pool(pool, 0)
                    inverse_std(pool, 1)
                    for e in range(1, E):
                        experts_pool(pool, e)

                @block.vector
                def _(dve):
                    chain = Chain(dve)
                    for n in range(len(proj)):
                        dve.wait_ge(S["proj_hi"], n + 1)
                        nc.vector.scalar_tensor_tensor(out=proj_target(n, 1), in0=proj_src(n),
                                                       scalar=proj_scale(n), in1=proj_target(n, 0),
                                                       op0=ALU.mult, op1=ALU.subtract).then_inc(S["proj_lo"], 1)
                        if n == AT_CHOOSE:
                            choose(dve, chain)
                        if n == AT_ONEHOT + 1:
                            copy_onehot(dve)
                        if n == AT_ADD2:
                            dve.wait_ge(y_out, 64 * i + 16)
                            add_bias2(dve)

                    for s in range(PIPE):
                        w = window_at(s, LAG_OC)
                        if w is not None:
                            rows = ROWS[w % 2]
                            dve.wait_ge(S["pv_mm"], 4 * w + 4)
                            if w >= 2:
                                dve.wait_ge(S["o_ready"], w - 1)
                            nc.vector.tensor_copy(o_raw[0:rows, w % 2], o_bank(rows)).then_inc(S["o_copied"], 1)
                        if s < UNITS:
                            half = unit_of(s)[1]
                            rows, kn = ROWS[half], KWN[half]
                            ps = split_heads(bank[s % SR][0:rows, 0:HU * kn])
                            least = smin[0:rows, s % XR, :]
                            dve.wait_ge(S["scores_mm"], s + 1)
                            nc.vector.tensor_reduce(least, ps, AX_X, ALU.min).then_inc(S["min_ready"], 1)
                        u = s - LAG_LO
                        if 0 <= u < UNITS:
                            half = unit_of(u)[1]
                            nk, n = (128, 69)[half], HU * KWN[half]
                            dve.wait_ge(S["pt_hi"], u + 1)
                            nc.vector.tensor_tensor(pt[0:nk, u % PR, 1, 0:n], bank[T_BANK + u % TR][0:nk, 0:n],
                                                    pt[0:nk, u % PR, 0, 0:n], ALU.subtract
                                                    ).then_inc(S["pt_lo"], 1)
                        w = window_at(s, LAG_OR)
                        if w is not None:
                            rows = ROWS[w % 2]
                            dve.wait_ge(S["o_copied"], w + 1)
                            if w >= 2:
                                dve.wait_ge(S["o_ready"], w - 1)
                            nc.vector.reciprocal(o_rcp[0:rows, w % 2], o_raw[0:rows, w % 2, :, :, 2 * HD:VW]
                                                 ).then_inc(S["o_rcp_ready"], 1)
                        n = patch_at(s - PATCH_LAG)
                        if n is not None and (n + 1) % (2 * PATCH_PARTS) == 0:
                            half = n // (2 * PATCH_PARTS)
                            if half == 0:
                                dve.wait_ge(S["h_moved"], 1)
                            dve.wait_ge(S["patch_mm"], 2 * half + 2)
                            add_token_bias(half).then_inc(S["embedded"], 1)
                        if s == LN_STEPS[0]:
                            dve.wait_ge(S["embedded"], 2)
                            for tt in range(4):
                                moments(chain, h_next, tt)
                        if s == LN_STEPS[1]:
                            for tt in range(4):
                                normalise(dve, 0, h_next, z, "z1_ready", tt)
                        if turned_at(s - OT_LO):
                            e, blk = turned_at(s - OT_LO)
                            r0, third = ((0, 1), (64, 2))[blk]
                            dve.wait_ge(S["ot_hi"], 2 * e + blk + 1)
                            nc.vector.tensor_tensor(ot[r0:128, e, third, :], bank[OT_BANK][r0:128, 0:TP],
                                                    ot[r0:128, e, 2 * blk, :], ALU.subtract
                                                    ).then_inc(S["ot_lo"], 1)

                    low_of(dve, OUT_BANK, zt1, "z1t_hi", "z1t_lo")
                    for tt in range(4):
                        rows = tile_of(tt)[3]
                        sg, gu, gu_psum = sig[0:rows, tt, :], gated[0:rows, tt, :], bank[GU_BANKS[tt]]
                        dve.wait_ge(S["sig_ready"], tt + 1)
                        chain(nc.vector.tensor_scalar(sg, sg, 1.0, None, ALU.add))
                        chain(nc.vector.reciprocal(sg, sg))
                        chain(nc.vector.scalar_tensor_tensor(out=gu, in0=gu_psum[0:rows, 0:D], scalar=INV,
                                                             in1=sg, op0=ALU.mult, op1=ALU.mult))
                        chain(nc.vector.scalar_tensor_tensor(out=gu, in0=gu_psum[0:rows, D:2 * D],
                                                             scalar=INV, in1=gu, op0=ALU.mult, op1=ALU.mult))
                        chain(nc.vector.tensor_tensor(h[0:rows, tt, :], h[0:rows, tt, :], gu, ALU.add))
                        moments(chain, h, tt)
                    for e in range(E):
                        if e == E - 1:
                            low_of(dve, 0, zt2, "z2t_hi", "z2t_lo")
                        experts_dve(dve, e)
                        if e == 0:
                            for tt in range(4):
                                normalise(dve, 1, h, z, "z2_ready", tt)

            nc.all_engine_barrier(sems_to_clear=per_turn)

        with nc.Block() as block:
            @block.sync
            def _(sp):
                store(sp, STEPS - 1)
                sp.wait_ge(y_out, 64 * STEPS + 80)

            @block.tensor
            def _(pe):
                logits()
                turn_onehot(pe)
                bias2(pe)
                pe.wait_ge(S["acc_ready"], 2)
                experts_pe(pe, False)

            @block.scalar
            def _(act):
                act.wait_ge(x_in, 16 * (STEPS + 2))
                experts_act(act)

            @block.gpsimd
            def _(pool):
                for e in range(E):
                    experts_pool(pool, e)

            @block.vector
            def _(dve):
                choose(dve, Chain(dve))
                copy_onehot(dve)
                dve.wait_ge(y_out, 64 * STEPS + 16)
                add_bias2(dve)
                for e in range(E):
                    experts_dve(dve, e)


def layouts(x, cls_tok, L0_tok_W_proj, L0_tok_b_proj, L0_attn_wq, L0_attn_wk, L0_attn_wv, L0_attn_wo,
            L0_attn_w_gate, L0_attn_w_up, L0_ffn_gate_w, L0_ffn_gate_b, L0_ffn_gate_center, L0_ffn_w1,
            L0_ffn_b1, L0_ffn_w2, L0_ffn_b2):
    import numpy as np
    f = np.float32

    def rows(a, kb):
        return a.reshape(-1, kb, *a.shape[1:]).swapaxes(0, 1)

    def packed(a):
        return np.stack([a[0:128], np.concatenate([a[128:D], a[128:D]])], 1)

    p = x.reshape(IMGS, 3, 14, 16, 14, 16).transpose(1, 3, 5, 0, 2, 4).reshape(PATCH, STEPS, PAIR, TOK - 1)
    x_t = np.zeros((STEPS, 128, PKT, PAIR, TOK), f)
    x_t[..., 1:] = p.reshape(PKT, 128, STEPS, PAIR, TOK - 1).transpose(2, 1, 0, 3, 4)
    tok_bias = np.empty((128, 2, D), f)
    tok_bias[:] = L0_tok_b_proj
    tok_bias[0, 0] = cls_tok[0, 0]
    gate_bc = np.empty((128, 2, E), f)
    gate_bc[:, 0] = L0_ffn_gate_b
    gate_bc[:, 1] = L0_ffn_gate_center
    order = np.empty((QKP, 4), int)
    for g in range(G):
        j0, row = place_of(g)
        order[j0:j0 + HP, row] = HP * g + np.arange(HP)
    columns = (2 * HD * order.reshape(-1, 1) + np.arange(2 * HD)).reshape(-1)
    wq, wk, wv = (w.transpose(2, 0, 1).reshape(D, E * D) for w in (L0_attn_wq, L0_attn_wk, L0_attn_wv))
    wqkv = np.stack([packed(w) for w in (wq[:, columns], wk[:, columns], wv)], 1)
    wgu = np.concatenate([L0_attn_w_gate.T, L0_attn_w_up.T], 1)
    masks = []
    for half in range(2):
        q = QW[half] + np.arange(128)[:, None]
        k = KW0[half] + np.arange(KWN[half])[None, :]
        m = np.where((q - k >= 0) & (q - k < WIN), 0.0, MASKED)
        masks.append(np.tile(m, (1, HU)))
    c = np.ascontiguousarray
    return dict(
        x_t=x_t.reshape(STEPS, 128, PKT, TP),
        wp=c(rows(L0_tok_W_proj.T, 128).reshape(128, -1)),
        tok_bias=tok_bias,
        wqkv=c(wqkv.reshape(128, -1)),
        wo=c(rows(packed(L0_attn_wo.transpose(2, 1, 0)).transpose(2, 3, 1, 0).reshape(D, E, 256), KB)),
        wgu=c(rows(wgu, KB)),
        gate_w=c(packed(L0_ffn_gate_w).reshape(128, -1)),
        gate_bc=gate_bc,
        w1=c(packed(L0_ffn_w1.transpose(1, 0, 2)).reshape(128, -1)),
        b1=c(L0_ffn_b1.reshape(E, HM, 128).transpose(2, 0, 1)),
        w2=c(L0_ffn_w2.reshape(E, HM, 128, D).transpose(2, 0, 1, 3).reshape(128, -1)),
        b2=c(L0_ffn_b2),
        ident=np.eye(128, dtype=f),
        mask_id=(MASK_ID * np.eye(128)).astype(np.float16),
        masks=np.concatenate(masks, 1).astype(np.float16),
    )


def kernel(**inputs):
    import numpy as np
    from concourse import bacc
    from concourse.bass_utils import run_bass_kernel_spmd

    arrays = layouts(**{k: np.asarray(a) for k, a in inputs.items()})
    nc = bacc.Bacc("TRN2", target_bir_lowering=False, num_devices=1)
    args = {n: nc.dram_tensor(f"{n}_dram", a.shape, mybir.dt.from_np(a.dtype), kind="ExternalInput").ap()
            for n, a in arrays.items()}
    out = nc.dram_tensor("out_dram", (STEPS, PAIR, TOK, D), F32, kind="ExternalOutput").ap()
    vit_layer(nc, **args, out=out)
    r = run_bass_kernel_spmd(nc, [{f"{n}_dram": a for n, a in arrays.items()}], core_ids=[0])
    return r.results[0]["out_dram"].reshape(IMGS, TOK, D)
```
